# Optimizing a Trainium2 kernel written in Bass

```python
import numpy as np
import jax
import jax.numpy as jnp

def _softmax(x, axis=-1):
    return jax.nn.softmax(x, axis=axis)

def _gelu(x):
    return jax.nn.gelu(x, approximate=True)

def _silu(x):
    return jax.nn.silu(x)

def _sigmoid(x):
    return jax.nn.sigmoid(x)

def _layernorm(x, axis=-1, eps=1e-05):
    m = jnp.mean(x, axis=axis, keepdims=True)
    v = jnp.var(x, axis=axis, keepdims=True)
    return (x - m) / jnp.sqrt(v + eps)

def _scatter_add(tgt, idx, src, axis=0):
    return tgt.at[idx].add(src)

def _segment_sum(src, seg, n):
    return jax.ops.segment_sum(src, seg, n)
kernel_name = 'mk_early_fusion_d1_tok_img1024_r4_52950c'

def setup_inputs(seed: int=0):
    np.random.seed(seed)
    _w = jnp.asarray

    def _rec_inputs():
        import jax
        import jax.numpy as jnp
        _rk = jax.random.key(seed)
        x = -0.000222058 + 0.999998 * jax.random.normal(jax.random.fold_in(_rk, 1), (128, 3, 64, 64), jnp.float32)
        txt = 0.000354947 + 1.41246 * jax.random.normal(jax.random.fold_in(_rk, 2), (128, 32, 256), jnp.float32)
        return (x, txt)
    x, txt = _rec_inputs()

    def _L0_tok_setup():
        import jax, jax.numpy as jnp
        import numpy as np
        IMG, PS, C, OUT = (64, 16, 3, 256)
        NP = IMG // PS
        IN_FEAT = C * PS * PS
        key = jax.random.key(seed)
        k1, k2, k3, k4 = jax.random.split(key, 4)
        x = jax.random.normal(k1, (128, C, IMG, IMG), dtype=jnp.float32)
        W = jax.random.normal(k2, (OUT, IN_FEAT), dtype=jnp.float32) / np.sqrt(IN_FEAT)
        b = jax.random.normal(k3, (OUT,), dtype=jnp.float32) * 0.01
        pos_emb = jax.random.normal(k4, (NP * NP, OUT), dtype=jnp.float32)
        return {'x': x, 'W': W, 'b': b, 'pos_emb': pos_emb}
    _L0_tok_all = _L0_tok_setup()
    _L0_tok_in = {k: v for k, v in _L0_tok_all.items() if k in ('W', 'b', 'pos_emb')}
    del _L0_tok_all

    def _L0_attn_setup():
        import jax, jax.numpy as jnp
        import numpy as np
        B, S, E = (4, 512, 256)
        HIDDEN = 256
        HEADS = 16
        key = jax.random.key(seed)
        k0, k1, k2, k3, k4 = jax.random.split(key, 5)
        inputs = jax.random.normal(k0, (B, S, E), dtype=jnp.float32)
        W_qkv = jax.random.normal(k1, (E, 3 * HIDDEN), dtype=jnp.float32) * 0.02
        b_qkv = jnp.zeros((3 * HIDDEN,), dtype=jnp.float32)
        W_out = jax.random.normal(k2, (HIDDEN, HIDDEN), dtype=jnp.float32) * 0.02
        b_out = jnp.zeros((HIDDEN,), dtype=jnp.float32)
        return {'inputs': inputs, 'W_qkv': W_qkv, 'b_qkv': b_qkv, 'W_out': W_out, 'b_out': b_out}
    _L0_attn_all = _L0_attn_setup()
    _L0_attn_in = {k: v for k, v in _L0_attn_all.items() if k in ('W_qkv', 'b_qkv', 'W_out', 'b_out')}
    del _L0_attn_all

    def _L0_ffn_setup():
        import jax, jax.numpy as jnp
        import numpy as np
        LN_EPS = 0.001
        EPS = 1e-05
        QB = 128.0

        def ste_round(x):
            return x + jax.lax.stop_gradient(jnp.round(x) - x)
        key = jax.random.key(seed)
        k1, k2 = jax.random.split(key)
        x = jax.random.normal(k1, (4, 2048, 256), dtype=jnp.float32)
        weight = jax.random.normal(k2, (256, 256), dtype=jnp.float32) * 0.02
        ln_gamma = jnp.ones((256,), dtype=jnp.float32)
        ln_beta = jnp.zeros((256,), dtype=jnp.float32)
        return {'x': x, 'weight': weight, 'ln_gamma': ln_gamma, 'ln_beta': ln_beta}
    _L0_ffn_all = _L0_ffn_setup()
    _L0_ffn_in = {k: v for k, v in _L0_ffn_all.items() if k in ('weight', 'ln_gamma', 'ln_beta')}
    del _L0_ffn_all
    return {'x': x, 'txt': txt, 'L0_tok_W': _L0_tok_in['W'], 'L0_tok_b': _L0_tok_in['b'], 'L0_tok_pos_emb': _L0_tok_in['pos_emb'], 'L0_attn_W_qkv': _L0_attn_in['W_qkv'], 'L0_attn_b_qkv': _L0_attn_in['b_qkv'], 'L0_attn_W_out': _L0_attn_in['W_out'], 'L0_attn_b_out': _L0_attn_in['b_out'], 'L0_ffn_weight': _L0_ffn_in['weight'], 'L0_ffn_ln_gamma': _L0_ffn_in['ln_gamma'], 'L0_ffn_ln_beta': _L0_ffn_in['ln_beta']}

def reference(x, txt, L0_tok_W, L0_tok_b, L0_tok_pos_emb, L0_attn_W_qkv, L0_attn_b_qkv, L0_attn_W_out, L0_attn_b_out, L0_ffn_weight, L0_ffn_ln_gamma, L0_ffn_ln_beta):
    import jax
    import jax.numpy as jnp

    def _L0_tok_ref(x, W, b, pos_emb):
        import jax, jax.numpy as jnp
        import numpy as np
        IMG, PS, C, OUT = (64, 16, 3, 256)
        NP = IMG // PS
        IN_FEAT = C * PS * PS
        B = x.shape[0]
        p = x.reshape(B, C, NP, PS, NP, PS).transpose(0, 1, 2, 4, 3, 5)
        p = p.transpose(0, 2, 3, 1, 4, 5)
        p = p.reshape(B, NP * NP, IN_FEAT)
        out = jnp.einsum('bnf,of->bno', p, W) + b + pos_emb
        return out

    def _L0_attn_ref(inputs, W_qkv, b_qkv, W_out, b_out):
        import jax, jax.numpy as jnp
        import numpy as np
        B, S, E = (4, 512, 256)
        HIDDEN = 256
        HEADS = 16
        Bv, Sv, Ev = inputs.shape
        x = inputs @ W_qkv + b_qkv
        x = x.reshape(Bv, HEADS, Sv, -1)
        q, k, v = jnp.split(x, 3, axis=-1)
        scale = (2 * HIDDEN) ** (-0.5)
        qk = jnp.einsum('bhse,bhte->bhst', q, k) * scale
        mask = jnp.triu(jnp.full((Sv, Sv), -jnp.inf, dtype=qk.dtype), k=1)
        attn = jax.nn.softmax(qk + mask, axis=-1)
        sa = jnp.einsum('bhst,bhte->bhse', attn, v).reshape(Bv, Sv, -1)
        return sa @ W_out + b_out

    def _L0_ffn_ref(x, weight, ln_gamma, ln_beta):
        import jax, jax.numpy as jnp
        import numpy as np
        LN_EPS = 0.001
        EPS = 1e-05
        QB = 128.0

        def ste_round(x):
            return x + jax.lax.stop_gradient(jnp.round(x) - x)
        mu = jnp.mean(x, axis=-1, keepdims=True)
        var = jnp.var(x, axis=-1, keepdims=True)
        xn = (x - mu) * jax.lax.rsqrt(var + LN_EPS) * ln_gamma + ln_beta
        beta = jnp.mean(jnp.abs(weight))
        w_q = jnp.clip(ste_round(weight / (beta + EPS)), -1.0, 1.0)
        gamma = jnp.max(jnp.abs(xn))
        xq = jnp.clip(xn * QB / gamma, -QB + EPS, QB - EPS)
        y = jnp.einsum('bsd,du->bsu', xq, w_q)
        return y * (gamma * beta / QB)
    h = _L0_tok_ref(x, L0_tok_W, L0_tok_b, L0_tok_pos_emb)
    h = jnp.concatenate([h, txt], axis=1)
    h = h + _L0_attn_ref(_layernorm(h, axis=-1), L0_attn_W_qkv, L0_attn_b_qkv, L0_attn_W_out, L0_attn_b_out)
    h = h + _L0_ffn_ref(_layernorm(h, axis=-1), L0_ffn_weight, L0_ffn_ln_gamma, L0_ffn_ln_beta)
    return h

_drawn_inputs = setup_inputs


def setup_inputs(seed=0):
    import zlib

    import numpy as np

    out = dict(_drawn_inputs(seed))
    spreads = {'L0_attn_b_qkv': (0.0, 0.8),
     'L0_attn_b_out': (0.0, 0.1),
     'L0_ffn_ln_gamma': (1.0, 0.535),
     'L0_ffn_ln_beta': (0.0, 0.564)}
    factors = {'L0_tok_b': 8.0}
    for name, (base, spread) in spreads.items():
        noise = np.random.default_rng([zlib.crc32(name.encode()), seed]).standard_normal(out[name].shape)
        drawn = base * np.exp(spread * noise) if base else spread * noise
        out[name] = jnp.asarray(drawn.astype(out[name].dtype))
    for name, factor in factors.items():
        out[name] = (out[name] * factor).astype(out[name].dtype)
    return out
```

```python
from contextlib import ExitStack

import concourse.bass as bass
from concourse import mybir

F32 = mybir.dt.float32
ALU = mybir.AluOpType
ACT = mybir.ActivationFunctionType
AX = mybir.AxisListType

P = 128
ST = 16
R = 3
J = 16
D = 16
S = R * J
SP2 = 64
E = 256
QKV = 3 * E
KT = E // P
KX = 768 // P
UNITS = 8
SLOTS = 8
SCALE = float(2 * E) ** -0.5
MASKED = -3.0e38
LN_EPS = 1e-5
FFN_LN_EPS = 1e-3
QB = 128.0
CLIP = QB - 1e-5


def build(nc, x_patches, txt_whole, txt_part, tok_w, tok_b, pos, w_qkv, b_qkv, w_out, b_out, w_ffn,
          ln_gamma, ln_beta, out):
    with ExitStack() as ctx:
        def sb(name, shape, dt=F32):
            return ctx.enter_context(nc.sbuf_tensor(name, shape, dt))

        def sem(name):
            return ctx.enter_context(nc.semaphore(name))

        H = sb("H", [P, ST, R * E])
        XNT = sb("XNT", [P, ST, KT * R * P])
        wq_sb = sb("wq_sb", [P, KT, QKV])
        wo_sb = sb("wo_sb", [P, KT, E])
        wf_sb = sb("wf_sb", [P, KT, E])
        tw_sb = sb("tw_sb", [P, KX, E])
        bq_sb = sb("bq_sb", [P, QKV])
        bo_sb = sb("bo_sb", [P, E])
        posb = sb("posb", [P, E])
        gam = sb("gam", [P, KT])
        bet = sb("bet", [P, KT])
        mask = sb("mask", [P, S])
        ident = sb("ident", [P, P])
        half = sb("half", [P, R])
        pmax = sb("pmax", [P, ST])
        small = sb("small", [P, 16])
        xp = [sb(f"xp{i}", [P, KX, P]) for i in range(2)]
        emb = [sb(f"emb{i}", [P, E]) for i in range(2)]
        st1 = sb("st1", [P, R, 6])
        mv1 = sb("mv1", [P, R, 2])
        ve1 = sb("ve1", [P, R])
        rs1 = sb("rs1", [P, R])
        z1 = sb("z1", [P, R, E])
        hT = sb("hT", [P, KT, R * P])
        qkv = sb("qkv", [P, R, QKV])
        qT = [sb(f"qT{i}", [P, 32 * S + 16]) for i in range(2)]
        kT = [sb(f"kT{i}", [P, 32 * S + 16]) for i in range(2)]
        vT = [sb(f"vT{i}", [P, 64, D + 1]) for i in range(2)]
        Sm = [sb(f"Sm{i}", [P, SLOTS, S]) for i in range(2)]
        mx = [sb(f"mx{i}", [P, SLOTS]) for i in range(2)]
        Pr = [sb(f"Pr{i}", [P, SLOTS, SP2]) for i in range(4)]
        PT = [sb(f"PT{i}", [P, 4, P]) for i in range(2)]
        OT = sb("OT", [P, 32, S])
        O = sb("O", [P, S, 32])
        rc = sb("rc", [P, S])
        sa = sb("sa", [P, R, E])
        st2 = sb("st2", [P, R, 6])
        mv2 = sb("mv2", [P, R, 2])
        ve2 = sb("ve2", [P, 4, R])
        rs2 = sb("rs2", [P, R])
        z2 = sb("z2", [P, R, E])
        saT = z2[:].rearrange("p r e -> p (r e)").rearrange("p (k m) -> p k m", k=KT)
        zero = z2[:, 0, 0:P]

        psS = [ctx.enter_context(nc.psum_tensor(f"psS{i}", [P, SLOTS, SP2], F32)) for i in range(2)]
        psO = [ctx.enter_context(nc.psum_tensor(f"psO{i}", [P, 512], F32)) for i in range(2)]
        psP = ctx.enter_context(nc.psum_tensor("psP", [P, 4, P], F32))
        psA = [ctx.enter_context(nc.psum_tensor(f"psA{i}", [P, 512], F32)) for i in range(2)]
        psC = ctx.enter_context(nc.psum_tensor("psC", [P, 512], F32))

        w_in = sem("w_in")
        s_zero, s_one, s_const, s_prep, s_pool0 = sem("s_zero"), sem("s_one"), sem("s_const"), sem("s_prep"), sem("s_pool0")
        ld_x = [sem(f"ld_x{i}") for i in range(2)]
        ld_t = [sem(f"ld_t{i}") for i in range(2)]
        ld_e = [sem(f"ld_e{i}") for i in range(2)]
        e_mm, e_ev = sem("e_mm"), sem("e_ev")
        bn1, av1, pw1, r1, zz1 = sem("bn1"), sem("av1"), sem("pw1"), sem("r1"), sem("zz1")
        h_mm, h_ev = sem("h_mm"), sem("h_ev")
        q_mm, q_ev, qk_t = sem("q_mm"), sem("q_ev"), sem("qk_t")
        v_mm, v_ev = sem("v_mm"), sem("v_ev")
        s_mm, s_ev, s_max, s_sub, s_exp = sem("s_mm"), sem("s_ev"), sem("s_max"), sem("s_sub"), sem("s_exp")
        p_mm, p_ev, o_mm, o_ev = sem("p_mm"), sem("p_ev"), sem("o_mm"), sem("o_ev")
        o_t, o_rc, o_sa = sem("o_t"), sem("o_rc"), sem("o_sa")
        c_mm, c_ev, w_mm, w_ev, h_bias = sem("c_mm"), sem("c_ev"), sem("w_mm"), sem("w_ev"), sem("h_bias")
        bn2, av2, pw2, r2, zz2 = sem("bn2"), sem("av2"), sem("pw2"), sem("r2"), sem("zz2")
        t_mm, t_ev, a_max = sem("t_mm"), sem("t_ev"), sem("a_max")
        g_max, g_all, g_sc = sem("g_max"), sem("g_all"), sem("g_sc")
        x_sc, x_cl, y_mm, y_ev = sem("x_sc"), sem("x_cl"), sem("y_mm"), sem("y_ev")
        st_o = [sem(f"st_o{i}") for i in range(2)]

        def after(s, per, k):
            return s * per + k

        def alone(eng):
            eng.nop(nofuse=True)

        def A_bank(par, use):
            return psA[(par + use) % 2]

        def A_free(eng, s, use):
            if use < 2:
                if not (isinstance(s, int) and s == 0):
                    eng.wait_ge(v_ev, after(s - 1, 4, 3 + use))
            elif use == 2:
                eng.wait_ge(e_ev, after(s, 1, 1))
            elif use < 5:
                eng.wait_ge(h_ev, after(s, 2, use - 2))
            elif use < 11:
                eng.wait_ge(q_ev, after(s, 6, use - 4))
            else:
                eng.wait_ge(v_ev, after(s, 4, use - 10))

        def unit(s, par, n, prev, cur):
            if n >= 0:
                return (s, par, n) if cur else None
            return (s - 1, 1 - par, n + UNITS) if prev else None

        def half_count(s, n):
            return s * 2 + n // 4

        def pe_iteration(pe, s, par, prev, cur, nxt):
            for t in range(8):
                if cur:
                    c, hh = t % 4, t // 4
                    if t == 0:
                        pe.wait_ge(qk_t, after(s, 6, 6))
                    if t >= 2 or prev:
                        pe.wait_ge(s_ev, after(s, 8, t - 1))
                    alone(pe)
                    for slot in range(SLOTS):
                        for v in range(2):
                            g = 16 * hh + 2 * slot + v
                            mm = nc.tensor.matmul(psS[t % 2][64 * v:64 * v + 64, slot, 0:S],
                                                  qT[par][32 * c:32 * c + D, g * S:g * S + SP2],
                                                  kT[par][32 * c:32 * c + D, g * S:g * S + S],
                                                  start=True, stop=True)
                    mm.then_inc(s_mm, 1)
                if u := unit(s, par, t - 2, prev, cur):
                    us, up, un = u
                    pe.wait_ge(s_exp, after(us, 8, un + 1))
                    if un > 0 or not (isinstance(us, int) and us == 0):
                        pe.wait_ge(p_ev, after(us, 8, un))
                    for k in range(4):
                        mm = nc.tensor.transpose(psP[:, k, :], Pr[un % 4][:, 2 * k:2 * k + 2, :].rearrange("p a b -> p (a b)"),
                                                 ident[:])
                    mm.then_inc(p_mm, 1)
                if nxt:
                    pe_stage_a(pe, s + 1, 1 - par, t)
                if u := unit(s, par, t - 3, prev, cur):
                    us, up, un = u
                    c, hh = un % 4, un // 4
                    pe.wait_ge(p_ev, after(us, 8, un + 1))
                    if un == 0:
                        pe.wait_ge(v_ev, after(us, 4, 4))
                    if c == 0 and not (isinstance(us, int) and us == 0 and hh == 0):
                        pe.wait_ge(o_ev, half_count(us, un))
                    alone(pe)
                    for hu in range(2):
                        for kk in range(4):
                            for v in range(2):
                                g = c * 16 + (4 * hh + kk) * 2 + v
                                mm = nc.tensor.matmul(psO[hu][32 * c:32 * c + D + 1, (2 * kk + v) * S:(2 * kk + v + 1) * S],
                                                      vT[up][64 * hu:64 * hu + S, g, :],
                                                      PT[un % 2][64 * hu:64 * hu + S, kk, 64 * v:64 * v + S],
                                                      start=True, stop=True)
                    mm.then_inc(o_mm, 1)
                if prev:
                    pe_stage_c(pe, s - 1, t)

        def pe_stage_a(pe, s, par, t):
            if t == 0:
                pe.wait_ge(ld_x[par], half_of(s, par))
                A_free(pe, s, 0)
                for k in range(KX):
                    mm = nc.tensor.matmul(A_bank(par, 0)[:, 0:E], xp[par][:, k, :], tw_sb[:, k, :],
                                          start=(k == 0), stop=(k == KX - 1))
                mm.then_inc(e_mm, 1)
            if t == 3:
                pe.wait_ge(zz1, after(s, 3, 3))
                for k in range(KT):
                    A_free(pe, s, 1 + k)
                    for r in range(R):
                        mm = nc.tensor.transpose(A_bank(par, 1 + k)[:, r * P:(r + 1) * P], z1[:, r, k * P:(k + 1) * P],
                                                 ident[:])
                    mm.then_inc(h_mm, 1)
            if t in (4, 5, 6):
                r = t - 4
                pe.wait_ge(h_ev, after(s, 2, 2))
                for ch in range(2):
                    A_free(pe, s, 3 + 2 * r + ch)
                    for k in range(KT):
                        mm = nc.tensor.matmul(A_bank(par, 3 + 2 * r + ch)[:, 0:384], hT[:, k, r * P:(r + 1) * P],
                                              wq_sb[:, k, ch * 384:(ch + 1) * 384], start=(k == 0), stop=(k == KT - 1))
                    mm.then_inc(q_mm, 1)
            if t == 7:
                pe.wait_ge(q_ev, after(s, 6, 6))
                vcol = qkv[:].rearrange("p r (j c) -> p (r j) c", c=S)
                for q in range(4):
                    A_free(pe, s, 9 + q)
                    alone(pe)
                    for i in range(4):
                        e = 32 + 4 * q + i
                        mm = nc.tensor.transpose(A_bank(par, 9 + q)[0:S, i * P:(i + 1) * P], vcol[:, :, e], ident[:])
                    mm.then_inc(v_mm, 1)

        def half_of(s, par):
            return (s - par) * 8 + 16

        def pe_stage_c(pe, s, t):
            if t == 4:
                pe.wait_ge(o_sa, after(s, 1, 1))
                for k in range(KT):
                    if k > 0:
                        pe.wait_ge(c_ev, after(s, 2, 1))
                    elif not (isinstance(s, int) and s == 0):
                        pe.wait_ge(t_ev, after(s - 1, 2, 2))
                    for r in range(R):
                        mm = nc.tensor.transpose(psC[:, r * P:(r + 1) * P], sa[:, r, k * P:(k + 1) * P], ident[:])
                    mm.then_inc(c_mm, 1)
            if t == 5:
                pe.wait_ge(c_ev, after(s, 2, 2))
                for r in range(R):
                    if r > 0:
                        pe.wait_ge(w_ev, after(s, 3, r))
                    for k in range(KT):
                        mm = nc.tensor.matmul(psC[:, 0:E], saT[:, k, r * P:(r + 1) * P], wo_sb[:, k, :],
                                              start=(k == 0), stop=(k == KT - 1))
                    mm.then_inc(w_mm, 1)
            if t == 7:
                pe.wait_ge(zz2, after(s, 3, 3))
                for k in range(KT):
                    pe.wait_ge(*((w_ev, after(s, 3, 3)) if k == 0 else (t_ev, after(s, 2, 1))))
                    for r in range(R):
                        mm = nc.tensor.transpose(psC[:, r * P:(r + 1) * P], z2[:, r, k * P:(k + 1) * P], ident[:])
                    mm.then_inc(t_mm, 1)

        def act_iteration(act, s, par, prev, cur, nxt):
            for t in range(8):
                if u := unit(s, par, t - 2, prev, cur):
                    us, up, un = u
                    act.wait_ge(p_mm, after(us, 8, un + 1))
                    if un >= 2 or not (isinstance(us, int) and us == 0):
                        act.wait_ge(o_mm, after(us, 8, un - 1))
                    nc.scalar.activation(PT[un % 2][:], psP[:], ACT.Copy).then_inc(p_ev, 1)
                if nxt and t == 3:
                    if not (isinstance(s, int) and s == -1):
                        act.wait_ge(q_mm, after(s, 6, 6))
                    for k in range(KT):
                        act.wait_ge(h_mm, after(s + 1, 2, k + 1))
                        nc.scalar.activation(hT[:, k, :], A_bank(1 - par, 1 + k)[:, 0:R * P], ACT.Copy).then_inc(h_ev, 1)
                if nxt and t == 7:
                    if not (isinstance(s, int) and s < 1):
                        act.wait_ge(o_mm, after(s - 1, 8, 8))
                    for q in range(4):
                        act.wait_ge(v_mm, after(s + 1, 4, q + 1))
                        src = A_bank(1 - par, 9 + q)[0:S, :].rearrange("p (e g u v) -> p u g v e", e=4, u=2, v=2)
                        for hu in range(2):
                            dst = vT[1 - par][64 * hu:64 * hu + S, :, 4 * q:4 * q + 4].rearrange(
                                "p (g v) e -> p g v e", v=2)
                            a = nc.scalar.activation(dst, src[:, hu], ACT.Copy)
                        a.then_inc(v_ev, 1)
                if cur:
                    act.wait_ge(s_sub, after(s, 8, t + 1))
                    nc.scalar.activation(Pr[t % 4][:, :, 0:S], Pr[t % 4][:, :, 0:S], ACT.Exp).then_inc(s_exp, 1)
                if (u := unit(s, par, t - 3, prev, cur)) and u[2] % 4 == 3:
                    us, up, un = u
                    hh = un // 4
                    act.wait_ge(o_mm, after(us, 8, un + 1))
                    if hh == 0 and not (isinstance(us, int) and us == 0):
                        act.wait_ge(o_t, after(us - 1, 1, 1))
                    for hu in range(2):
                        dst = OT[:, 16 * hh:16 * hh + 16, :].rearrange("p (k u v) s -> p u k v s", u=2, v=2)[:, hu]
                        src = psO[hu][:, 0:8 * S].rearrange("p (k v s) -> p k v s", k=4, v=2)
                        a = nc.scalar.activation(dst, src, ACT.Copy)
                    a.then_inc(o_ev, 1)
                if prev and t == 4:
                    if not (isinstance(s, int) and s == 1):
                        act.wait_ge(t_mm, after(s - 2, 2, 2))
                    for k in range(KT):
                        act.wait_ge(c_mm, after(s - 1, 2, k + 1))
                        nc.scalar.activation(saT[:, k, :], psC[:, 0:R * P], ACT.Copy).then_inc(c_ev, 1)
                if prev and t == 7:
                    for k in range(KT):
                        act.wait_ge(t_mm, after(s - 1, 2, k + 1))
                        dst = XNT[:, bass.ds(s - 1, 1), k * R * P:(k + 1) * R * P]
                        nc.scalar.activation(dst, psC[:, 0:R * P].unsqueeze(1), ACT.Identity, bias=bet[:, k:k + 1],
                                             scale=gam[:, k:k + 1]).then_inc(t_ev, 1)

        def pool_iteration(pool, s, par, prev, cur, nxt):
            for t in range(8):
                if cur:
                    pool.wait_ge(s_max, after(s, 8, t + 1))
                    if t >= 4 or prev:
                        pool.wait_ge(p_mm, after(s, 8, t - 3))
                    nc.gpsimd.tensor_tensor(Pr[t % 4][:, :, 0:S], Sm[t % 2][:],
                                            mx[t % 2][:].unsqueeze(2).to_broadcast([P, SLOTS, S]),
                                            ALU.subtract).then_inc(s_sub, 1)
                if nxt and t == 2:
                    pool.wait_ge(av1, after(s + 1, 3, 3))
                    alone(pool)
                    nc.gpsimd.tensor_scalar(ve1[:], mv1[:, :, 1], LN_EPS, None, ALU.add).then_inc(pw1, 1)
                    pool.wait_ge(pw1, after(s + 1, 1, 1))
                    if not (isinstance(s, int) and s == -1):
                        pool.wait_ge(zz1, after(s, 3, 3))
                    nc.gpsimd.tensor_tensor(rs1[:], ve1[:], half[:], ALU.pow).then_inc(r1, 1)
                if prev and t == 6:
                    pool.wait_ge(av2, after(s - 1, 3, 3))
                    alone(pool)
                    v = mv2[:, :, 1]
                    steps = [
                        lambda: nc.gpsimd.tensor_scalar(ve2[:, 0, :], v, LN_EPS, None, ALU.add),
                        lambda: nc.gpsimd.tensor_tensor(ve2[:, 1, :], ve2[:, 0, :], half[:], ALU.pow),
                        lambda: nc.gpsimd.tensor_tensor(ve2[:, 2, :], ve2[:, 1, :], ve2[:, 1, :], ALU.mult),
                        lambda: nc.gpsimd.tensor_tensor(ve2[:, 2, :], ve2[:, 2, :], v, ALU.mult),
                        lambda: nc.gpsimd.tensor_scalar(ve2[:, 2, :], ve2[:, 2, :], FFN_LN_EPS, None, ALU.add),
                        lambda: nc.gpsimd.tensor_tensor(ve2[:, 3, :], ve2[:, 2, :], half[:], ALU.pow),
                    ]
                    for k, step in enumerate(steps):
                        step().then_inc(pw2, 1)
                        pool.wait_ge(pw2, after(s - 1, 6, k + 1))
                        alone(pool)
                    if not (isinstance(s, int) and s == 1):
                        pool.wait_ge(zz2, after(s - 2, 3, 3))
                    nc.gpsimd.tensor_tensor(rs2[:], ve2[:, 1, :], ve2[:, 3, :], ALU.mult).then_inc(r2, 1)

        def dve_iteration(dve, s, par, prev, cur, nxt):
            n, p = s + 1, 1 - par
            for t in range(8):
                if nxt and t == 1:
                    dve.wait_ge(e_mm, after(n, 1, 1))
                    if not (isinstance(s, int) and s < 1):
                        dve.wait_ge(ld_e[p], (s - 1 - p) * 24 + 48)
                    nc.vector.tensor_tensor(emb[p][:], A_bank(p, 0)[:, 0:E], posb[:], ALU.add).then_inc(e_ev, 1)
                if cur:
                    dve.wait_ge(s_mm, after(s, 8, t + 1))
                    if t >= 2 or prev:
                        dve.wait_ge(s_sub, after(s, 8, t - 1))
                    nc.vector.scalar_tensor_tensor(Sm[t % 2][:], psS[t % 2][:, :, 0:S], SCALE,
                                                   mask[:].unsqueeze(1).to_broadcast([P, SLOTS, S]),
                                                   ALU.mult, ALU.add).then_inc(s_ev, 1)
                    dve.wait_ge(s_ev, after(s, 8, t + 1))
                    nc.vector.tensor_reduce(mx[t % 2][:], Sm[t % 2][:], AX.X, ALU.max).then_inc(s_max, 1)
                if nxt and t == 2:
                    dve.wait_ge(ld_e[p], (n - p) * 24 + 48)
                    dve.wait_ge(ld_t[p], (n - p) * 16 + 32)
                    stats(dve, n, st1, mv1, bn1, av1)
                if nxt and t == 3:
                    dve.wait_ge(r1, after(n, 1, 1))
                    if not (isinstance(s, int) and s == -1):
                        dve.wait_ge(h_mm, after(s, 2, 2))
                    for r in range(R):
                        nc.vector.tensor_scalar(z1[:, r, :].unsqueeze(1), H[:, bass.ds(n, 1), r * E:(r + 1) * E], mv1[:, r, 0:1],
                                                rs1[:, r:r + 1], ALU.subtract, ALU.mult).then_inc(zz1, 1)
                if nxt and t in (4, 5, 6):
                    r = t - 4
                    if not (isinstance(s, int) and s == -1):
                        if r == 0:
                            dve.wait_ge(v_mm, after(s, 4, 4))
                            dve.wait_ge(qk_t, after(s, 6, 6))
                    for ch in range(2):
                        dve.wait_ge(q_mm, after(n, 6, 2 * r + ch + 1))
                        nc.vector.tensor_tensor(qkv[:, r, ch * 384:(ch + 1) * 384], A_bank(p, 3 + 2 * r + ch)[:, 0:384],
                                                bq_sb[:, ch * 384:(ch + 1) * 384], ALU.add).then_inc(q_ev, 1)
                    if r == 0 and not (isinstance(s, int) and s < 1):
                        dve.wait_ge(s_mm, after(s - 1, 8, 8))
                    dve.wait_ge(q_ev, after(n, 6, 2 * r + 2))
                    rows = qkv[:, r, :].rearrange("p (j c) -> p j c", c=S)
                    for dst, c0 in ((qT[p], 0), (kT[p], 16)):
                        view = dst[:, 0:32 * S].rearrange("p (g s) -> p s g", s=S)[:, r * J:(r + 1) * J, :]
                        nc.vector.transpose(view, rows[:, :, c0:c0 + 32]).then_inc(qk_t, 1)
                if prev and t == 3:
                    dve.wait_ge(o_ev, after(s - 1, 2, 2))
                    nc.vector.transpose(O[:], OT[:].rearrange("p g s -> p s g")).then_inc(o_t, 1)
                    dve.wait_ge(o_t, after(s - 1, 1, 1))
                    nc.vector.reciprocal(rc[:], O[:, :, D]).then_inc(o_rc, 1)
                    dve.wait_ge(o_rc, after(s - 1, 1, 1))
                    if not (isinstance(s, int) and s == 1):
                        dve.wait_ge(c_mm, after(s - 2, 2, 2))
                    nc.vector.tensor_tensor(sa[:].rearrange("p r (j e) -> p (r j) e", e=D), O[:, :, 0:D],
                                            rc[:].unsqueeze(2).to_broadcast([P, S, D]), ALU.mult).then_inc(o_sa, 1)
                if prev and t == 5:
                    for r in range(R):
                        dve.wait_ge(w_mm, after(s - 1, 3, r + 1))
                        h = H[:, bass.ds(s - 1, 1), r * E:(r + 1) * E]
                        nc.vector.tensor_tensor(h, h, psC[:, 0:E].unsqueeze(1), ALU.add).then_inc(w_ev, 1)
                if prev and t == 6:
                    dve.wait_ge(w_ev, after(s - 1, 3, 3))
                    h = H[:, bass.ds(s - 1, 1), :].rearrange("p a (r e) -> p (a r) e", r=R)
                    nc.vector.tensor_tensor(h, h, bo_sb[:].unsqueeze(1).to_broadcast([P, R, E]),
                                            ALU.add).then_inc(h_bias, 1)
                    dve.wait_ge(h_bias, after(s - 1, 1, 1))
                    stats(dve, s - 1, st2, mv2, bn2, av2)
                if prev and t == 7:
                    dve.wait_ge(r2, after(s - 1, 1, 1))
                    if not (isinstance(s, int) and s == 1):
                        dve.wait_ge(t_mm, after(s - 2, 2, 2))
                    for r in range(R):
                        nc.vector.tensor_scalar(z2[:, r, :].unsqueeze(1), H[:, bass.ds(s - 1, 1), r * E:(r + 1) * E],
                                                mv2[:, r, 0:1], rs2[:, r:r + 1], ALU.subtract, ALU.mult).then_inc(zz2, 1)
                    dve.wait_ge(t_ev, after(s - 1, 2, 2))
                    nc.vector.tensor_reduce(pmax[:, bass.ds(s - 1, 1)], XNT[:, bass.ds(s - 1, 1), :], AX.X, ALU.max,
                                            apply_absolute_value=True).then_inc(a_max, 1)

        def stats(dve, s, st, mv, bn, av):
            alone(dve)
            for r in range(R):
                nc.vector.bn_stats(st[:, r, :], H[:, bass.ds(s, 1), r * E:(r + 1) * E]).then_inc(bn, 1)
            dve.wait_ge(bn, after(s, 3, 3))
            alone(dve)
            for r in range(R):
                nc.vector.bn_aggr(mv[:, r, :], st[:, r, :]).then_inc(av, 1)

        def sp_iteration(sp, s, par, prev, cur, nxt):
            if not nxt:
                return
            n, p = s + 1, 1 - par
            if not (isinstance(s, int) and s < 1):
                sp.wait_ge(e_mm, after(s - 1, 1, 1))
                sp.wait_ge(ld_t[p], (s - 1 - p) * 16 + 32)
            sp.dma_start(xp[p][:].rearrange("p k m -> p (k m)").unsqueeze(1),
                         x_patches[bass.ds(n, 1)].rearrange("s p f -> p s f")).then_inc(ld_x[p], 16)
            sp.dma_start(H[48:P, bass.ds(n, 1), :], txt_whole[bass.ds(n, 1)].rearrange("s p f -> p s f")).then_inc(ld_t[p], 16)
            sp.dma_start(H[40:48, bass.ds(n, 1), E:3 * E], txt_part[bass.ds(n, 1)].rearrange("s p f -> p s f")).then_inc(ld_t[p], 16)
            sp.wait_ge(e_ev, after(n, 1, 1))
            for r, (a, b) in enumerate(((0, 48), (48, 88), (88, 128))):
                sp.dma_start(H[0:b - a, bass.ds(n, 1), r * E:(r + 1) * E], emb[p][a:b, :].unsqueeze(1)).then_inc(ld_e[p], 16)

        def pipeline(eng, iteration):
            iteration(eng, -1, 1, False, False, True)
            iteration(eng, 0, 0, False, True, True)
            with eng.Fori(0, (ST - 2) // 2) as i:
                iteration(eng, i * 2 + 1, 1, True, True, True)
                iteration(eng, i * 2 + 2, 0, True, True, True)
            iteration(eng, ST - 1, 1, True, True, False)
            iteration(eng, ST, 0, True, False, False)

        with nc.Block() as block:
            @block.sync
            def _(sp):
                def load(dst, src):
                    sp.dma_start(dst, src).then_inc(w_in, 16)
                load(tw_sb[:], tok_w.rearrange("(k p) n -> p k n", p=P))
                for r, (a, b) in enumerate(((0, 48), (48, 88), (88, 128))):
                    rows = pos[r:16:3, :]
                    load(posb[a:b, :], rows.unsqueeze(1).to_broadcast([(b - a) // 8, 8, E]))
                load(emb[0][:], tok_b.partition_broadcast(P))
                load(wq_sb[:], w_qkv.rearrange("(k p) n -> p k n", p=P))
                load(bq_sb[:], b_qkv.partition_broadcast(P))
                load(wo_sb[:], w_out.rearrange("(k p) n -> p k n", p=P))
                load(bo_sb[:], b_out.partition_broadcast(P))
                load(wf_sb[:], w_ffn.rearrange("(k p) n -> p k n", p=P))
                with nc.allow_non_contiguous_dma(reason="256 values"):
                    load(gam[:], ln_gamma.rearrange("(k p) -> p k", p=P))
                    load(bet[:], ln_beta.rearrange("(k p) -> p k", p=P))

            @block.gpsimd
            def _(pool):
                nc.gpsimd.memset(zero, 0.0).then_inc(s_zero, 1)
                nc.gpsimd.memset(mask[:], 0.0).then_inc(s_zero, 1)
                pool.wait_ge(s_zero, 2)
                nc.gpsimd.affine_select(out=ident[:], in_=zero, compare_op=ALU.not_equal, fill=1.0, base=0,
                                        pattern=[[-1, P]], channel_multiplier=1).then_inc(s_const, 1)
                for v in range(2):
                    pool.wait_ge(s_const, v + 1)
                    m = mask[64 * v:64 * v + 64, :]
                    nc.gpsimd.affine_select(out=m, in_=m, compare_op=ALU.is_ge, fill=MASKED, base=0,
                                            pattern=[[-1, S]], channel_multiplier=1).then_inc(s_const, 1)
                pool.wait_ge(s_const, 3)
                pool.wait_ge(s_prep, 1)
                nc.gpsimd.partition_all_reduce(small[:, 1:2], small[:, 0:1], P, bass.bass_isa.ReduceOp.add).then_inc(s_pool0, 1)

            @block.vector
            def _(dve):
                prep = [0]

                def step(ins):
                    prep[0] += 1
                    ins.then_inc(s_prep, 1)
                    dve.wait_ge(s_prep, prep[0])

                dve.wait_ge(w_in, 16 * 12)
                step(nc.vector.tensor_reduce(small[:, 0:1], wf_sb[:].rearrange("p k n -> p (k n)"), AX.X, ALU.add,
                                             apply_absolute_value=True))
                for b in range(2):
                    nc.vector.memset(qT[b][:, 32 * S:], 0.0).then_inc(s_one, 1)
                    nc.vector.memset(vT[b][:, :, D:D + 1], 1.0).then_inc(s_one, 1)
                    nc.vector.memset(psO[b][:], 0.0).then_inc(s_one, 1)
                for b in range(4):
                    nc.vector.memset(Pr[b][:], 0.0).then_inc(s_one, 1)
                nc.vector.memset(half[:], -0.5).then_inc(s_one, 1)
                step(nc.vector.tensor_tensor(posb[:], posb[:], emb[0][:], ALU.add))
                dve.wait_ge(s_pool0, 1)
                step(nc.vector.tensor_scalar(small[:, 2:3], small[:, 1:2], 1.0 / (E * E), None, ALU.mult))
                step(nc.vector.tensor_scalar(small[:, 3:4], small[:, 2:3], 1e-5, 0.5, ALU.add, ALU.mult))
                step(nc.vector.tensor_scalar(small[:, 4:5], small[:, 3:4], -1.0, None, ALU.mult))
                flat = wf_sb[:].rearrange("p k n -> p (k n)")
                below = hT[:].rearrange("p k n -> p (k n)")[:, 0:KT * E]
                step(nc.vector.tensor_scalar(below, flat, small[:, 4:5], None, ALU.is_lt))
                step(nc.vector.scalar_tensor_tensor(flat, flat, small[:, 3:4], below, ALU.is_gt, ALU.subtract))

        with nc.Block() as block:
            @block.sync
            def _(sp):
                pipeline(sp, sp_iteration)

            @block.tensor
            def _(pe):
                pipeline(pe, pe_iteration)

            @block.scalar
            def _(act):
                pipeline(act, act_iteration)

            @block.gpsimd
            def _(pool):
                pipeline(pool, pool_iteration)

            @block.vector
            def _(dve):
                pipeline(dve, dve_iteration)

        xq = [xp[i][:].rearrange("p k m -> p (k m)")[:, 0:KT * R * P] for i in range(2)]
        yo = [z1, z2]
        ybanks = [psS[0], psS[1], psP, psA[0], psA[1], psC]
        ybank = [b[:].rearrange("p a b -> p (a b)") if len(b[:].shape) == 3 else b[:] for b in ybanks]

        with nc.Block() as block:
            @block.gpsimd
            def _(pool):
                pool.wait_ge(g_max, 1)
                nc.gpsimd.partition_all_reduce(small[:, 6:7], small[:, 5:6], P, bass.bass_isa.ReduceOp.max).then_inc(g_all, 1)

            @block.vector
            def _(dve):
                nc.vector.tensor_reduce(small[:, 5:6], pmax[:], AX.X, ALU.max).then_inc(g_max, 1)
                dve.wait_ge(g_all, 1)
                nc.vector.reciprocal(small[:, 7:8], small[:, 6:7]).then_inc(g_sc, 1)
                nc.vector.tensor_scalar(small[:, 8:9], small[:, 6:7], small[:, 2:3], 1.0 / QB, ALU.mult,
                                        ALU.mult).then_inc(g_sc, 1)
                dve.wait_ge(g_sc, 2)

                def dve_pair(i):
                    for b in range(2):
                        s = i * 2 + b
                        if not isinstance(i, int):
                            dve.wait_ge(y_mm, s * 3 - 3)
                        nc.vector.tensor_scalar(xq[b].unsqueeze(1), XNT[:, bass.ds(s, 1), :], QB, small[:, 7:8],
                                                ALU.mult, ALU.mult).then_inc(x_sc, 1)
                        dve.wait_ge(x_sc, s + 1)
                        nc.vector.tensor_scalar(xq[b], xq[b], CLIP, -CLIP, ALU.min, ALU.max).then_inc(x_cl, 1)
                        if not isinstance(i, int):
                            dve.wait_ge(st_o[b], i * 16)
                        for r in range(R):
                            dve.wait_ge(y_mm, s * 3 + r + 1)
                            nc.vector.scalar_tensor_tensor(yo[b][:, r, :].unsqueeze(1), ybank[3 * b + r][:, 0:E].unsqueeze(1),
                                                           small[:, 8:9], H[:, bass.ds(s, 1), r * E:(r + 1) * E],
                                                           ALU.mult, ALU.add).then_inc(y_ev, 1)

                dve_pair(0)
                with dve.Fori(1, ST // 2) as i:
                    dve_pair(i)

            @block.tensor
            def _(pe):
                def pe_pair(i):
                    for b in range(2):
                        s = i * 2 + b
                        pe.wait_ge(x_cl, s + 1)
                        if not isinstance(i, int):
                            pe.wait_ge(y_ev, s * 3 - 3)
                        for r in range(R):
                            for k in range(KT):
                                mm = nc.tensor.matmul(ybank[3 * b + r][:, 0:E], xq[b][:, (k * R + r) * P:(k * R + r + 1) * P],
                                                      wf_sb[:, k, :], start=(k == 0), stop=(k == KT - 1))
                            mm.then_inc(y_mm, 1)

                pe_pair(0)
                with pe.Fori(1, ST // 2) as i:
                    pe_pair(i)

            @block.sync
            def _(sp):
                with sp.Fori(0, ST // 2) as i:
                    for b in range(2):
                        s = i * 2 + b
                        sp.wait_ge(y_ev, s * 3 + 3)
                        sp.dma_start(out[bass.ds(s, 1)].rearrange("s p f -> p s f"),
                                     yo[b][:].rearrange("p r e -> p (r e)").unsqueeze(1)).then_inc(st_o[b], 16)
                for b in range(2):
                    sp.wait_ge(st_o[b], 16 * (ST // 2))


def kernel(x, txt, L0_tok_W, L0_tok_b, L0_tok_pos_emb, L0_attn_W_qkv, L0_attn_b_qkv, L0_attn_W_out, L0_attn_b_out,
           L0_ffn_weight, L0_ffn_ln_gamma, L0_ffn_ln_beta):
    import numpy as np
    import concourse.bacc as bacc
    from concourse.bass_utils import run_bass_kernel_spmd

    p = np.ascontiguousarray(x).reshape(ST, 8, 3, 4, 16, 4, 16).transpose(2, 4, 6, 0, 3, 5, 1)
    p = p.reshape(KX, P, ST, 16, 8)
    order = [n for r in range(R) for n in range(r, 16, R)]
    p = np.ascontiguousarray(p[:, :, :, order].transpose(2, 1, 0, 3, 4)).reshape(ST, P, KX * P)
    t = np.ascontiguousarray(txt).reshape(ST, 8, 32 * E)
    whole = np.ascontiguousarray(t[:, :, 2 * E:].reshape(ST, 8, 10, R * E).transpose(0, 2, 1, 3)).reshape(ST, 80, R * E)
    part = np.ascontiguousarray(t[:, :, 0:2 * E])
    arrays = {
        "x_patches": p, "txt_whole": whole, "txt_part": part, "tok_w": np.ascontiguousarray(np.transpose(L0_tok_W)),
        "tok_b": L0_tok_b, "pos": L0_tok_pos_emb, "w_qkv": L0_attn_W_qkv, "b_qkv": L0_attn_b_qkv,
        "w_out": L0_attn_W_out, "b_out": L0_attn_b_out, "w_ffn": L0_ffn_weight, "ln_gamma": L0_ffn_ln_gamma,
        "ln_beta": L0_ffn_ln_beta,
    }
    arrays = {n: np.ascontiguousarray(a) for n, a in arrays.items()}
    nc = bacc.Bacc("TRN2", target_bir_lowering=False, num_devices=1)
    args = [nc.dram_tensor(n, a.shape, mybir.dt.from_np(a.dtype), kind="ExternalInput").ap() for n, a in arrays.items()]
    args.append(nc.dram_tensor("out", (ST, P, R * E), F32, kind="ExternalOutput").ap())
    build(nc, *args)
    got = run_bass_kernel_spmd(nc, [arrays], core_ids=[0]).results[0]["out"]
    return np.ascontiguousarray(np.reshape(got, (ST, 16, 8, R * E)).transpose(0, 2, 1, 3)).reshape(128, 48, E)
```

```python
from contextlib import ExitStack

import concourse.bass as bass
from concourse import mybir

F32 = mybir.dt.float32
ALU = mybir.AluOpType
ACT = mybir.ActivationFunctionType
AX = mybir.AxisListType

P = 128
ST = 16
R = 3
J = 16
D = 16
S = R * J
SP2 = 64
E = 256
QKV = 3 * E
KT = E // P
KX = 768 // P
UNITS = 8
SLOTS = 8
SCALE = float(2 * E) ** -0.5
MASKED = -3.0e38
LN_EPS = 1e-5
FFN_LN_EPS = 1e-3
QB = 128.0
CLIP = QB - 1e-5


def build(nc, x_patches, txt_whole, txt_part, tok_w, tok_b, pos, w_qkv, b_qkv, w_out, b_out, w_ffn,
          ln_gamma, ln_beta, out):
    with ExitStack() as ctx:
        def sb(name, shape, dt=F32):
            return ctx.enter_context(nc.sbuf_tensor(name, shape, dt))

        def sem(name):
            return ctx.enter_context(nc.semaphore(name))

        H = sb("H", [P, ST, R * E])
        XNT = sb("XNT", [P, ST, KT * R * P])
        wq_sb = sb("wq_sb", [P, KT, QKV])
        wo_sb = sb("wo_sb", [P, KT, E])
        wf_sb = sb("wf_sb", [P, KT, E])
        tw_sb = sb("tw_sb", [P, KX, E])
        bq_sb = sb("bq_sb", [P, QKV])
        bo_sb = sb("bo_sb", [P, E])
        posb = sb("posb", [P, E])
        gam = sb("gam", [P, KT])
        bet = sb("bet", [P, KT])
        mask = sb("mask", [P, S])
        ident = sb("ident", [P, P])
        half = sb("half", [P, R])
        pmax = sb("pmax", [P, ST])
        small = sb("small", [P, 16])
        xp = [sb(f"xp{i}", [P, KX, P]) for i in range(2)]
        emb = [sb(f"emb{i}", [P, E]) for i in range(2)]
        st1 = sb("st1", [P, R, 6])
        mv1 = sb("mv1", [P, R, 2])
        ve1 = sb("ve1", [P, R])
        rs1 = sb("rs1", [P, R])
        z1 = sb("z1", [P, R, E])
        hT = sb("hT", [P, KT, R * P])
        qkv = sb("qkv", [P, R, QKV])
        qT = [sb(f"qT{i}", [P, 32 * S + 16]) for i in range(2)]
        kT = [sb(f"kT{i}", [P, 32 * S + 16]) for i in range(2)]
        vT = [sb(f"vT{i}", [P, 64, D + 1]) for i in range(2)]
        Sm = [sb(f"Sm{i}", [P, SLOTS, S]) for i in range(2)]
        mx = [sb(f"mx{i}", [P, SLOTS]) for i in range(2)]
        Pr = [sb(f"Pr{i}", [P, SLOTS, SP2]) for i in range(4)]
        PT = [sb(f"PT{i}", [P, 4, P]) for i in range(2)]
        OT = sb("OT", [P, 32, S])
        O = sb("O", [P, S, 32])
        rc = sb("rc", [P, S])
        sa = sb("sa", [P, R, E])
        st2 = sb("st2", [P, R, 6])
        mv2 = sb("mv2", [P, R, 2])
        ve2 = sb("ve2", [P, R])
        rs2 = sb("rs2", [P, R])
        z2 = sb("z2", [P, R, E])
        saT = z2[:].rearrange("p r e -> p (r e)").rearrange("p (k m) -> p k m", k=KT)
        zero = z2[:, 0, 0:P]

        psS = [ctx.enter_context(nc.psum_tensor(f"psS{i}", [P, SLOTS, SP2], F32)) for i in range(2)]
        psO = [ctx.enter_context(nc.psum_tensor(f"psO{i}", [P, 512], F32)) for i in range(2)]
        psP = ctx.enter_context(nc.psum_tensor("psP", [P, 4, P], F32))
        psA = [ctx.enter_context(nc.psum_tensor(f"psA{i}", [P, 512], F32)) for i in range(2)]
        psC = ctx.enter_context(nc.psum_tensor("psC", [P, 512], F32))

        w_tok, w_pos, w_att, w_ffn_in = sem("w_tok"), sem("w_pos"), sem("w_att"), sem("w_ffn_in")
        s_pos, s_abs = sem("s_pos"), sem("s_abs")
        s_zero, s_one, s_const, s_prep, s_pool0 = sem("s_zero"), sem("s_one"), sem("s_const"), sem("s_prep"), sem("s_pool0")
        ld_x = [sem(f"ld_x{i}") for i in range(2)]
        ld_t = [sem(f"ld_t{i}") for i in range(2)]
        ld_e = [sem(f"ld_e{i}") for i in range(2)]
        e_mm, e_ev = sem("e_mm"), sem("e_ev")
        bn1, av1, pw1, r1, zz1 = sem("bn1"), sem("av1"), sem("pw1"), sem("r1"), sem("zz1")
        h_mm, h_ev = sem("h_mm"), sem("h_ev")
        q_mm, q_ev, qk_t = sem("q_mm"), sem("q_ev"), sem("qk_t")
        v_mm, v_ev = sem("v_mm"), sem("v_ev")
        s_mm, s_ev, s_max, s_sub, s_exp = sem("s_mm"), sem("s_ev"), sem("s_max"), sem("s_sub"), sem("s_exp")
        p_mm, p_ev, o_mm, o_ev = sem("p_mm"), sem("p_ev"), sem("o_mm"), sem("o_ev")
        o_t, o_rc, o_sa = sem("o_t"), sem("o_rc"), sem("o_sa")
        c_mm, c_ev, w_mm, w_ev, h_bias = sem("c_mm"), sem("c_ev"), sem("w_mm"), sem("w_ev"), sem("h_bias")
        bn2, av2, pw2, r2, zz2 = sem("bn2"), sem("av2"), sem("pw2"), sem("r2"), sem("zz2")
        t_mm, t_ev, a_max = sem("t_mm"), sem("t_ev"), sem("a_max")
        g_max, g_all, g_sc = sem("g_max"), sem("g_all"), sem("g_sc")
        x_sc, x_cl, y_mm, y_ev = sem("x_sc"), sem("x_cl"), sem("y_mm"), sem("y_ev")
        st_o = [sem(f"st_o{i}") for i in range(2)]

        ONES = 12

        def after(s, per, k):
            return s * per + k

        def alone(eng):
            eng.nop(nofuse=True)

        def A_bank(par, use):
            return psA[(par + use) % 2]

        def A_free(eng, s, use, emb=True):
            if use < 2 or (use == 2 and not emb):
                if not (isinstance(s, int) and s == 0):
                    eng.wait_ge(v_ev, after(s - 1, 4, 3 + use % 2))
            elif use == 2:
                eng.wait_ge(e_ev, after(s + 1, 1, 1))
            elif use < 5:
                eng.wait_ge(h_ev, after(s, 2, use - 2))
            elif use < 11:
                eng.wait_ge(q_ev, after(s, 6, use - 4))
            else:
                eng.wait_ge(v_ev, after(s, 4, use - 10))

        def unit(s, par, n, prev, cur):
            if n >= 0:
                return (s, par, n) if cur else None
            return (s - 1, 1 - par, n + UNITS) if prev else None

        def half_count(s, n):
            return s * 2 + n // 4

        def pe_iteration(pe, s, par, prev, cur, nxt, emb):
            for t in range(8):
                if cur:
                    pe_scores(pe, s, par, t, 0, prev)
                pe_stages(pe, s, par, prev, nxt, emb, t, 0)
                if cur:
                    pe_scores(pe, s, par, t, 1, prev)
                pe_stages(pe, s, par, prev, nxt, emb, t, 1)
                if u := unit(s, par, t - 2, prev, cur):
                    pe_values(pe, *u)
                pe_stages(pe, s, par, prev, nxt, emb, t, 2)
                if u := unit(s, par, t - 1, prev, cur):
                    pe_turn(pe, *u)
                pe_stages(pe, s, par, prev, nxt, emb, t, 3)

        def pe_scores(pe, s, par, t, part, prev):
            c, hh = t % 4, t // 4
            if part == 0:
                if t == 0:
                    pe.wait_ge(qk_t, after(s, 6, 6))
                if t >= 2 or prev:
                    pe.wait_ge(s_ev, after(s, 8, t - 1))
                alone(pe)
            for slot in range(4 * part, 4 * part + 4):
                for v in range(2):
                    g = 16 * hh + 2 * slot + v
                    mm = nc.tensor.matmul(psS[t % 2][64 * v:64 * v + 64, slot, 0:S],
                                          qT[par][32 * c:32 * c + D, g * S:g * S + SP2],
                                          kT[par][32 * c:32 * c + D, g * S:g * S + S],
                                          start=True, stop=True)
            if part == 1:
                mm.then_inc(s_mm, 1)

        def pe_turn(pe, us, up, un):
            pe.wait_ge(s_exp, after(us, 8, un + 1))
            if un > 0 or not (isinstance(us, int) and us == 0):
                pe.wait_ge(p_ev, after(us, 8, un))
            for k in range(4):
                mm = nc.tensor.transpose(psP[:, k, :], Pr[un % 4][:, 2 * k:2 * k + 2, :].rearrange("p a b -> p (a b)"),
                                         ident[:])
            mm.then_inc(p_mm, 1)

        def pe_values(pe, us, up, un):
            c, hh = un % 4, un // 4
            pe.wait_ge(p_ev, after(us, 8, un + 1))
            if un == 0:
                pe.wait_ge(v_ev, after(us, 4, 4))
            if c == 0 and not (isinstance(us, int) and us == 0 and hh == 0):
                pe.wait_ge(o_ev, half_count(us, un))
            alone(pe)
            for hu in range(2):
                for kk in range(4):
                    for v in range(2):
                        g = c * 16 + (4 * hh + kk) * 2 + v
                        mm = nc.tensor.matmul(psO[hu][32 * c:32 * c + D + 1, (2 * kk + v) * S:(2 * kk + v + 1) * S],
                                              vT[up][64 * hu:64 * hu + S, g, :],
                                              PT[un % 2][64 * hu:64 * hu + S, kk, 64 * v:64 * v + S],
                                              start=True, stop=True)
            mm.then_inc(o_mm, 1)

        EMBED = [(0, 3), (1, 1)]
        NORM = (2, 0)
        PROJECT = [(2, 3), (3, 2), (4, 1), (5, 2), (6, 1), (6, 3)]
        VALUES = [(7, 1), (7, 3)]
        OUTPUTS = [(3, 1), (3, 3)]
        PROJECT_OUT = [(4, 0), (4, 2), (5, 0)]
        NORM2 = [(7, 0), (7, 2)]

        def pe_stages(pe, s, par, prev, nxt, emb, t, part):
            at = (t, part)
            n, p = s + 1, 1 - par
            if emb and at in EMBED:
                pe_embed(pe, s + 2, par, EMBED.index(at))
            if nxt and at == NORM:
                pe_norm(pe, n, p, emb)
            if prev and at in OUTPUTS:
                pe_turn_outputs(pe, s - 1, OUTPUTS.index(at))
            if nxt and at in PROJECT:
                pe_project(pe, n, p, PROJECT.index(at) // 2, PROJECT.index(at) % 2)
            if nxt and at in VALUES:
                pe_turn_values(pe, n, p, VALUES.index(at))
            if prev and at in PROJECT_OUT:
                pe_project_out(pe, s - 1, PROJECT_OUT.index(at))
            if prev and at in NORM2:
                pe_turn_norm(pe, s - 1, NORM2.index(at))

        def pe_embed(pe, s, par, part):
            if part == 0:
                pe.wait_ge(ld_x[par], (s - par) * 8 + 16)
                if not (isinstance(s, int) and s == 0):
                    A_free(pe, s - 1, 0)
            for k in range(part * KX // 2, (part + 1) * KX // 2):
                mm = nc.tensor.matmul(A_bank(1 - par, 0)[:, 0:E], xp[par][:, k, :], tw_sb[:, k, :],
                                      start=(k == 0), stop=(k == KX - 1))
            if part == 1:
                mm.then_inc(e_mm, 1)

        def pe_norm(pe, s, par, emb):
            pe.wait_ge(zz1, after(s, 3, 3))
            for k in range(KT):
                A_free(pe, s, 1 + k, emb)
                for r in range(R):
                    mm = nc.tensor.transpose(A_bank(par, 1 + k)[:, r * P:(r + 1) * P], z1[:, r, k * P:(k + 1) * P],
                                             ident[:])
                mm.then_inc(h_mm, 1)

        def pe_project(pe, s, par, r, ch):
            if (r, ch) == (0, 0):
                pe.wait_ge(h_ev, after(s, 2, 2))
            A_free(pe, s, 3 + 2 * r + ch)
            for k in range(KT):
                mm = nc.tensor.matmul(A_bank(par, 3 + 2 * r + ch)[:, 0:384], hT[:, k, r * P:(r + 1) * P],
                                      wq_sb[:, k, ch * 384:(ch + 1) * 384], start=(k == 0), stop=(k == KT - 1))
            mm.then_inc(q_mm, 1)

        def pe_turn_values(pe, s, par, part):
            if part == 0:
                pe.wait_ge(q_ev, after(s, 6, 6))
            rows = qkv[:].rearrange("p r (j c) -> p (r j) c", c=S)
            for q in range(2 * part, 2 * part + 2):
                A_free(pe, s, 9 + q)
                alone(pe)
                for i in range(4):
                    mm = nc.tensor.transpose(A_bank(par, 9 + q)[0:S, i * P:(i + 1) * P], rows[:, :, 2 * D + 4 * q + i],
                                             ident[:])
                mm.then_inc(v_mm, 1)

        def pe_turn_outputs(pe, s, k):
            if k > 0:
                pe.wait_ge(c_ev, after(s, 2, 1))
            else:
                pe.wait_ge(o_sa, after(s, 1, 1))
                if not (isinstance(s, int) and s == 0):
                    pe.wait_ge(t_ev, after(s - 1, 2, 2))
            for r in range(R):
                mm = nc.tensor.transpose(psC[:, r * P:(r + 1) * P], sa[:, r, k * P:(k + 1) * P], ident[:])
            mm.then_inc(c_mm, 1)

        def pe_project_out(pe, s, r):
            pe.wait_ge(*((c_ev, after(s, 2, 2)) if r == 0 else (w_ev, after(s, 3, r))))
            for k in range(KT):
                mm = nc.tensor.matmul(psC[:, 0:E], saT[:, k, r * P:(r + 1) * P], wo_sb[:, k, :],
                                      start=(k == 0), stop=(k == KT - 1))
            mm.then_inc(w_mm, 1)

        def pe_turn_norm(pe, s, k):
            if k == 0:
                pe.wait_ge(zz2, after(s, 3, 3))
                pe.wait_ge(w_ev, after(s, 3, 3))
            else:
                pe.wait_ge(t_ev, after(s, 2, 1))
            for r in range(R):
                mm = nc.tensor.transpose(psC[:, r * P:(r + 1) * P], z2[:, r, k * P:(k + 1) * P], ident[:])
            mm.then_inc(t_mm, 1)

        def act_iteration(act, s, par, prev, cur, nxt, emb):
            for t in range(8):
                if nxt and t == 2:
                    act_norm1(act, s + 1, 1 - par)
                if (u := unit(s, par, t - 2, prev, cur)) and u[2] % 4 == 3:
                    act_half(act, *u)
                if prev and t == 3:
                    act_outputs(act, s - 1, 0)
                if prev and t == 7:
                    act_norm2(act, s - 1, 0)
                if nxt and t == 7:
                    act_values(act, s + 1, 1 - par, 0)
                if u := unit(s, par, t - 1, prev, cur):
                    us, up, un = u
                    act.wait_ge(p_mm, after(us, 8, un + 1))
                    if un >= 2 or not (isinstance(us, int) and us == 0):
                        act.wait_ge(o_mm, after(us, 8, un - 1))
                    nc.scalar.activation(PT[un % 2][:], psP[:], ACT.Copy).then_inc(p_ev, 1)
                if prev and t == 7:
                    act_norm2(act, s - 1, 1)
                if cur:
                    act.wait_ge(s_sub, after(s, 8, t + 1))
                    nc.scalar.activation(Pr[t % 4][:, :, 0:S], Pr[t % 4][:, :, 0:S], ACT.Exp).then_inc(s_exp, 1)
                if prev and t == 3:
                    act_outputs(act, s - 1, 1)
                if nxt and t == 7:
                    act_values(act, s + 1, 1 - par, 1)

        def act_norm1(act, s, par):
            if not (isinstance(s, int) and s == 0):
                act.wait_ge(q_mm, after(s - 1, 6, 6))
            for k in range(KT):
                act.wait_ge(h_mm, after(s, 2, k + 1))
                nc.scalar.activation(hT[:, k, :], A_bank(par, 1 + k)[:, 0:R * P], ACT.Copy).then_inc(h_ev, 1)

        def act_values(act, s, par, part):
            if part == 0 and not (isinstance(s, int) and s < 2):
                act.wait_ge(o_mm, after(s - 2, 8, 8))
            for q in range(2 * part, 2 * part + 2):
                act.wait_ge(v_mm, after(s, 4, q + 1))
                src = A_bank(par, 9 + q)[0:S, :].rearrange("p (e g u v) -> p u g v e", e=4, u=2, v=2)
                for hu in range(2):
                    dst = vT[par][64 * hu:64 * hu + S, :, 4 * q:4 * q + 4].rearrange("p (g v) e -> p g v e", v=2)
                    a = nc.scalar.activation(dst, src[:, hu], ACT.Copy)
                a.then_inc(v_ev, 1)

        def act_half(act, us, up, un):
            hh = un // 4
            act.wait_ge(o_mm, after(us, 8, un + 1))
            if hh == 0 and not (isinstance(us, int) and us == 0):
                act.wait_ge(o_t, after(us - 1, 1, 1))
            for hu in range(2):
                dst = OT[:, 16 * hh:16 * hh + 16, :].rearrange("p (k u v) s -> p u k v s", u=2, v=2)[:, hu]
                src = psO[hu][:, 0:8 * S].rearrange("p (k v s) -> p k v s", k=4, v=2)
                a = nc.scalar.activation(dst, src, ACT.Copy)
            a.then_inc(o_ev, 1)

        def act_outputs(act, s, k):
            if k == 0 and not (isinstance(s, int) and s == 0):
                act.wait_ge(t_mm, after(s - 1, 2, 2))
            act.wait_ge(c_mm, after(s, 2, k + 1))
            nc.scalar.activation(saT[:, k, :], psC[:, 0:R * P], ACT.Copy).then_inc(c_ev, 1)

        def act_norm2(act, s, k):
            act.wait_ge(t_mm, after(s, 2, k + 1))
            dst = XNT[:, bass.ds(s, 1), k * R * P:(k + 1) * R * P]
            nc.scalar.activation(dst, psC[:, 0:R * P].unsqueeze(1), ACT.Identity, bias=bet[:, k:k + 1],
                                 scale=gam[:, k:k + 1]).then_inc(t_ev, 1)

        def pool_iteration(pool, s, par, prev, cur, nxt, emb):
            for t in range(8):
                if cur:
                    pool.wait_ge(s_max, after(s, 8, t + 1))
                    if t >= 4 or prev:
                        pool.wait_ge(p_mm, after(s, 8, t - 3))
                    nc.gpsimd.tensor_tensor(Pr[t % 4][:, :, 0:S], Sm[t % 2][:],
                                            mx[t % 2][:].unsqueeze(2).to_broadcast([P, SLOTS, S]),
                                            ALU.subtract).then_inc(s_sub, 1)
                if nxt and t == 0:
                    power(pool, s + 1, av1, mv1, ve1, 1.0, LN_EPS, pw1, zz1, rs1, r1)
                if nxt and t == 3:
                    pool.wait_ge(zz1, after(s + 1, 3, 3))
                    h = H[:, bass.ds(s + 1, 1), :].rearrange("p a (r e) -> p (a r) e", r=R)
                    nc.gpsimd.tensor_tensor(h, h, bo_sb[:].unsqueeze(1).to_broadcast([P, R, E]),
                                            ALU.add).then_inc(h_bias, 1)
                if prev and t == 5:
                    power(pool, s - 1, av2, mv2, ve2, 1.0 + FFN_LN_EPS, FFN_LN_EPS * LN_EPS, pw2, zz2, rs2, r2)

        def power(pool, s, av, mv, ve, a, b, done, used, rs, ready):
            pool.wait_ge(av, after(s, 3, 3))
            alone(pool)
            nc.gpsimd.tensor_scalar(ve[:], mv[:, :, 1], a, b, ALU.mult, ALU.add).then_inc(done, 1)
            pool.wait_ge(done, after(s, 1, 1))
            if not (isinstance(s, int) and s == 0):
                pool.wait_ge(used, after(s - 1, 3, 3))
            nc.gpsimd.tensor_tensor(rs[:], ve[:], half[:], ALU.pow).then_inc(ready, 1)

        def dve_iteration(dve, s, par, prev, cur, nxt, emb):
            n, p = s + 1, 1 - par
            for t in range(8):
                if cur:
                    dve.wait_ge(s_mm, after(s, 8, t + 1))
                    if t >= 2 or prev:
                        dve.wait_ge(s_sub, after(s, 8, t - 1))
                    nc.vector.scalar_tensor_tensor(Sm[t % 2][:], psS[t % 2][:, :, 0:S], SCALE,
                                                   mask[:].unsqueeze(1).to_broadcast([P, SLOTS, S]),
                                                   ALU.mult, ALU.add).then_inc(s_ev, 1)
                    dve.wait_ge(s_ev, after(s, 8, t + 1))
                    nc.vector.tensor_reduce(mx[t % 2][:], Sm[t % 2][:], AX.X, ALU.max).then_inc(s_max, 1)
                if nxt and t == 0:
                    dve.wait_ge(ld_e[p], (n - p) * 24 + 48)
                    dve.wait_ge(ld_t[p], (n - p) * 16 + 32)
                    stats(dve, n, st1, mv1, bn1, av1)
                if nxt and t == 1:
                    dve.wait_ge(r1, after(n, 1, 1))
                    if not (isinstance(s, int) and s == -1):
                        dve.wait_ge(h_mm, after(s, 2, 2))
                    for r in range(R):
                        nc.vector.tensor_scalar(z1[:, r, :].unsqueeze(1), H[:, bass.ds(n, 1), r * E:(r + 1) * E], mv1[:, r, 0:1],
                                                rs1[:, r:r + 1], ALU.subtract, ALU.mult).then_inc(zz1, 1)
                if emb and t == 1:
                    dve_embed(dve, s + 2, par)
                if prev and t == 2:
                    dve.wait_ge(o_ev, after(s - 1, 2, 2))
                    nc.vector.transpose(O[:], OT[:].rearrange("p g s -> p s g")).then_inc(o_t, 1)
                    dve.wait_ge(o_t, after(s - 1, 1, 1))
                    nc.vector.reciprocal(rc[:], O[:, :, D]).then_inc(o_rc, 1)
                    dve.wait_ge(o_rc, after(s - 1, 1, 1))
                    if not (isinstance(s, int) and s == 1):
                        dve.wait_ge(c_mm, after(s - 2, 2, 2))
                    nc.vector.tensor_tensor(sa[:].rearrange("p r (j e) -> p (r j) e", e=D), O[:, :, 0:D],
                                            rc[:].unsqueeze(2).to_broadcast([P, S, D]), ALU.mult).then_inc(o_sa, 1)
                if nxt and t == 3:
                    dve_project(dve, n, p, 0, 0)
                    dve_project(dve, n, p, 0, 1)
                    dve_turn(dve, n, p, 0)
                if prev and t == 4:
                    dve_residual(dve, s - 1, 0)
                if nxt and t == 4:
                    dve_project(dve, n, p, 1, 0)
                if prev and t == 4:
                    dve_residual(dve, s - 1, 1)
                if prev and t == 5:
                    dve_residual(dve, s - 1, 2)
                    dve.wait_ge(w_ev, after(s - 1, 3, 3))
                    stats(dve, s - 1, st2, mv2, bn2, av2)
                if nxt and t == 5:
                    dve_project(dve, n, p, 1, 1)
                    dve_turn(dve, n, p, 1)
                if nxt and t == 6:
                    dve_project(dve, n, p, 2, 0)
                if prev and t == 6:
                    dve.wait_ge(r2, after(s - 1, 1, 1))
                    if not (isinstance(s, int) and s == 1):
                        dve.wait_ge(t_mm, after(s - 2, 2, 2))
                    for r in range(R):
                        nc.vector.tensor_scalar(z2[:, r, :].unsqueeze(1), H[:, bass.ds(s - 1, 1), r * E:(r + 1) * E],
                                                mv2[:, r, 0:1], rs2[:, r:r + 1], ALU.subtract, ALU.mult).then_inc(zz2, 1)
                if nxt and t == 6:
                    dve_project(dve, n, p, 2, 1)
                    dve_turn(dve, n, p, 2)
                if prev and t == 7:
                    dve.wait_ge(t_ev, after(s - 1, 2, 2))
                    nc.vector.tensor_reduce(pmax[:, bass.ds(s - 1, 1)], XNT[:, bass.ds(s - 1, 1), :], AX.X, ALU.max,
                                            apply_absolute_value=True).then_inc(a_max, 1)

        def dve_embed(dve, s, par):
            dve.wait_ge(e_mm, after(s, 1, 1))
            if not (isinstance(s, int) and s < 2):
                dve.wait_ge(ld_e[par], (s - par) * 24)
            nc.vector.tensor_tensor(emb[par][:], A_bank(1 - par, 0)[:, 0:E], posb[:], ALU.add).then_inc(e_ev, 1)

        def dve_residual(dve, s, r):
            dve.wait_ge(w_mm, after(s, 3, r + 1))
            if r == 0:
                dve.wait_ge(h_bias, after(s, 1, 1))
            h = H[:, bass.ds(s, 1), r * E:(r + 1) * E]
            nc.vector.tensor_tensor(h, h, psC[:, 0:E].unsqueeze(1), ALU.add).then_inc(w_ev, 1)

        def dve_project(dve, s, par, r, ch):
            if (r, ch) == (0, 0) and not (isinstance(s, int) and s == 0):
                dve.wait_ge(v_mm, after(s - 1, 4, 4))
                dve.wait_ge(qk_t, after(s - 1, 6, 6))
            dve.wait_ge(q_mm, after(s, 6, 2 * r + ch + 1))
            nc.vector.tensor_tensor(qkv[:, r, ch * 384:(ch + 1) * 384], A_bank(par, 3 + 2 * r + ch)[:, 0:384],
                                    bq_sb[:, ch * 384:(ch + 1) * 384], ALU.add).then_inc(q_ev, 1)

        def dve_turn(dve, s, par, r):
            if r == 0 and not (isinstance(s, int) and s < 2):
                dve.wait_ge(s_mm, after(s - 2, 8, 8))
            dve.wait_ge(q_ev, after(s, 6, 2 * r + 2))
            rows = qkv[:, r, :].rearrange("p (j c) -> p j c", c=S)
            for dst, c0 in ((qT[par], 0), (kT[par], D)):
                view = dst[:, 0:32 * S].rearrange("p (g s) -> p s g", s=S)[:, r * J:(r + 1) * J, :]
                nc.vector.transpose(view, rows[:, :, c0:c0 + 32]).then_inc(qk_t, 1)

        def stats(dve, s, st, mv, bn, av):
            alone(dve)
            for r in range(R):
                nc.vector.bn_stats(st[:, r, :], H[:, bass.ds(s, 1), r * E:(r + 1) * E]).then_inc(bn, 1)
            dve.wait_ge(bn, after(s, 3, 3))
            alone(dve)
            for r in range(R):
                nc.vector.bn_aggr(mv[:, r, :], st[:, r, :]).then_inc(av, 1)

        def load_x(sp, s, par):
            if not (isinstance(s, int) and s < 2):
                sp.wait_ge(e_mm, after(s - 2, 1, 1))
            sp.dma_start(xp[par][:].rearrange("p k m -> p (k m)").unsqueeze(1),
                         x_patches[bass.ds(s, 1)].rearrange("s p f -> p s f")).then_inc(ld_x[par], 16)

        def load_t(sp, s, par):
            if not (isinstance(s, int) and s < 2):
                sp.wait_ge(ld_t[par], (s - par) * 16)
            sp.dma_start(H[48:P, bass.ds(s, 1), :], txt_whole[bass.ds(s, 1)].rearrange("s p f -> p s f")).then_inc(ld_t[par], 16)
            sp.dma_start(H[40:48, bass.ds(s, 1), E:3 * E], txt_part[bass.ds(s, 1)].rearrange("s p f -> p s f")).then_inc(ld_t[par], 16)

        def place_e(sp, s, par):
            sp.wait_ge(e_ev, after(s, 1, 1))
            for r, (a, b) in enumerate(((0, 48), (48, 88), (88, 128))):
                sp.dma_start(H[0:b - a, bass.ds(s, 1), r * E:(r + 1) * E], emb[par][a:b, :].unsqueeze(1)).then_inc(ld_e[par], 16)

        def sp_iteration(sp, s, par, prev, cur, nxt, emb):
            if emb:
                if not (isinstance(s, int) and s + 3 >= ST):
                    load_x(sp, s + 3, 1 - par)
                load_t(sp, s + 2, par)
                place_e(sp, s + 2, par)

        def iterations(eng, iteration, after_first=None):
            iteration(eng, -1, 1, False, False, True, True)
            if after_first:
                after_first()
            iteration(eng, 0, 0, False, True, True, True)
            with eng.Fori(0, (ST - 4) // 2) as i:
                iteration(eng, i * 2 + 1, 1, True, True, True, True)
                iteration(eng, i * 2 + 2, 0, True, True, True, True)
            iteration(eng, ST - 3, 1, True, True, True, True)
            iteration(eng, ST - 2, 0, True, True, True, False)
            iteration(eng, ST - 1, 1, True, True, False, False)
            iteration(eng, ST, 0, True, False, False, False)

        xq = [xp[i][:].rearrange("p k m -> p (k m)")[:, 0:KT * R * P] for i in range(2)]
        ybanks = [psS[0], psS[1], psP, psA[0], psA[1], psC]
        ybank = [b[:].rearrange("p a b -> p (a b)") if len(b[:].shape) == 3 else b[:] for b in ybanks]

        def quantised(eng, one):
            for b in range(2):
                one(b, b)
            with eng.Fori(1, ST // 2) as i:
                for b in range(2):
                    one(i * 2 + b, b)

        with nc.Block() as block:
            @block.gpsimd
            def _(pool):
                nc.gpsimd.memset(zero, 0.0).then_inc(s_zero, 1)
                nc.gpsimd.memset(mask[:], 0.0).then_inc(s_zero, 1)
                pool.wait_ge(s_zero, 2)
                nc.gpsimd.affine_select(out=ident[:], in_=zero, compare_op=ALU.not_equal, fill=1.0, base=0,
                                        pattern=[[-1, P]], channel_multiplier=1).then_inc(s_const, 1)
                for v in range(2):
                    pool.wait_ge(s_const, v + 1)
                    m = mask[64 * v:64 * v + 64, :]
                    nc.gpsimd.affine_select(out=m, in_=m, compare_op=ALU.is_ge, fill=MASKED, base=0,
                                            pattern=[[-1, S]], channel_multiplier=1).then_inc(s_const, 1)

                def mean():
                    pool.wait_ge(s_abs, 1)
                    nc.gpsimd.partition_all_reduce(small[:, 1:2], small[:, 0:1], P,
                                                   bass.bass_isa.ReduceOp.add).then_inc(s_pool0, 1)

                pool.wait_ge(s_one, ONES)
                pool.wait_ge(w_att, 16 * 4)
                iterations(pool, pool_iteration, mean)
                pool.wait_ge(g_max, 1)
                nc.gpsimd.partition_all_reduce(small[:, 6:7], small[:, 5:6], P, bass.bass_isa.ReduceOp.max).then_inc(g_all, 1)

            @block.scalar
            def _(act):
                act.wait_ge(s_one, ONES)
                act.wait_ge(w_ffn_in, 16 * 3)
                iterations(act, act_iteration)
                act.wait_ge(g_sc, 3)

                def act_scale(s, b):
                    if not isinstance(s, int):
                        act.wait_ge(y_mm, s * 3 - 3)
                    nc.scalar.activation(xq[b].unsqueeze(1), XNT[:, bass.ds(s, 1), :], ACT.Identity, bias=small[:, 9:10],
                                         scale=small[:, 10:11]).then_inc(x_sc, 1)

                quantised(act, act_scale)

            @block.vector
            def _(dve):
                for b in range(2):
                    nc.vector.memset(qT[b][:, 32 * S:], 0.0).then_inc(s_one, 1)
                    nc.vector.memset(vT[b][:, :, D:D + 1], 1.0).then_inc(s_one, 1)
                    nc.vector.memset(psO[b][:], 0.0).then_inc(s_one, 1)
                for b in range(4):
                    nc.vector.memset(Pr[b][:], 0.0).then_inc(s_one, 1)
                nc.vector.memset(half[:], -0.5).then_inc(s_one, 1)
                nc.vector.memset(small[:, 9:10], 0.0).then_inc(s_one, 1)
                dve.wait_ge(w_pos, 16 * 4)
                nc.vector.tensor_tensor(posb[:], posb[:], emb[1][:], ALU.add).then_inc(s_pos, 1)
                dve.wait_ge(s_pos, 1)
                dve_embed(dve, 0, 0)
                dve.wait_ge(w_ffn_in, 16 * 3)
                nc.vector.tensor_reduce(small[:, 0:1], wf_sb[:].rearrange("p k n -> p (k n)"), AX.X, ALU.add,
                                        apply_absolute_value=True).then_inc(s_abs, 1)
                dve.wait_ge(s_const, 3)
                dve.wait_ge(w_att, 16 * 4)
                iterations(dve, dve_iteration)

                dve.wait_ge(a_max, ST)
                nc.vector.tensor_reduce(small[:, 5:6], pmax[:], AX.X, ALU.max).then_inc(g_max, 1)

                prep = [0]

                def step(ins):
                    prep[0] += 1
                    ins.then_inc(s_prep, 1)
                    dve.wait_ge(s_prep, prep[0])

                dve.wait_ge(s_pool0, 1)
                dve.wait_ge(q_mm, 6 * ST)
                step(nc.vector.tensor_scalar(small[:, 2:3], small[:, 1:2], 1.0 / (E * E), None, ALU.mult))
                step(nc.vector.tensor_scalar(small[:, 3:4], small[:, 2:3], 1e-5, 0.5, ALU.add, ALU.mult))
                step(nc.vector.tensor_scalar(small[:, 4:5], small[:, 3:4], -1.0, None, ALU.mult))
                flat = wf_sb[:].rearrange("p k n -> p (k n)")
                below = hT[:].rearrange("p k n -> p (k n)")[:, 0:KT * E]
                step(nc.vector.tensor_scalar(below, flat, small[:, 4:5], None, ALU.is_lt))
                step(nc.vector.scalar_tensor_tensor(flat, flat, small[:, 3:4], below, ALU.is_gt, ALU.subtract))

                dve.wait_ge(g_all, 1)
                nc.vector.reciprocal(small[:, 7:8], small[:, 6:7]).then_inc(g_sc, 1)
                nc.vector.tensor_scalar(small[:, 8:9], small[:, 6:7], small[:, 2:3], 1.0 / QB, ALU.mult,
                                        ALU.mult).then_inc(g_sc, 1)
                dve.wait_ge(g_sc, 2)
                nc.vector.tensor_scalar(small[:, 10:11], small[:, 7:8], QB, None, ALU.mult).then_inc(g_sc, 1)

                def dve_clip(s, b):
                    dve.wait_ge(x_sc, s + 1)
                    nc.vector.tensor_scalar(xq[b], xq[b], CLIP, -CLIP, ALU.min, ALU.max).then_inc(x_cl, 1)

                def dve_add(s, b):
                    h = H[:, bass.ds(s, 1), :]
                    for r in range(R):
                        dve.wait_ge(y_mm, s * 3 + r + 1)
                        nc.vector.scalar_tensor_tensor(h[:, :, r * E:(r + 1) * E], ybank[3 * b + r][:, 0:E].unsqueeze(1),
                                                       small[:, 8:9], h[:, :, r * E:(r + 1) * E],
                                                       ALU.mult, ALU.add).then_inc(y_ev, 1)

                dve_clip(0, 0)
                dve_clip(1, 1)
                dve_add(0, 0)
                with dve.Fori(1, ST // 2) as i:
                    dve_clip(i * 2, 0)
                    dve_add(i * 2 - 1, 1)
                    dve_clip(i * 2 + 1, 1)
                    dve_add(i * 2, 0)
                dve_add(ST - 1, 1)

            @block.tensor
            def _(pe):
                pe.wait_ge(w_tok, 16)
                pe_embed(pe, 0, 0, 0)
                pe_embed(pe, 0, 0, 1)
                pe.wait_ge(s_const, 1)
                pe.wait_ge(s_one, ONES)
                pe.wait_ge(w_att, 16 * 4)
                iterations(pe, pe_iteration)

                pe.wait_ge(s_ev, 8 * ST)
                pe.wait_ge(p_ev, 8 * ST)
                pe.wait_ge(v_ev, 4 * ST)
                pe.wait_ge(t_ev, 2 * ST)

                def pe_one(s, b):
                    pe.wait_ge(x_cl, s + 1)
                    for r in range(R):
                        if not isinstance(s, int):
                            pe.wait_ge(y_ev, s * 3 - 5 + r)
                        for k in range(KT):
                            mm = nc.tensor.matmul(ybank[3 * b + r][:, 0:E], xq[b][:, (k * R + r) * P:(k * R + r + 1) * P],
                                                  wf_sb[:, k, :], start=(k == 0), stop=(k == KT - 1))
                        mm.then_inc(y_mm, 1)

                quantised(pe, pe_one)

            @block.sync
            def _(sp):
                sp.dma_start(tw_sb[:], tok_w.rearrange("(k p) n -> p k n", p=P)).then_inc(w_tok, 16)
                load_x(sp, 0, 0)
                sp.dma_start(emb[1][:], tok_b.partition_broadcast(P)).then_inc(w_pos, 16)
                for r, (a, b) in enumerate(((0, 48), (48, 88), (88, 128))):
                    rows = pos[r:16:3, :]
                    sp.dma_start(posb[a:b, :], rows.unsqueeze(1).to_broadcast([(b - a) // 8, 8, E])).then_inc(w_pos, 16)
                load_t(sp, 0, 0)
                sp.dma_start(wq_sb[:], w_qkv.rearrange("(k p) n -> p k n", p=P)).then_inc(w_att, 16)
                load_x(sp, 1, 1)
                sp.dma_start(bq_sb[:], b_qkv.partition_broadcast(P)).then_inc(w_att, 16)
                sp.dma_start(wo_sb[:], w_out.rearrange("(k p) n -> p k n", p=P)).then_inc(w_att, 16)
                sp.dma_start(bo_sb[:], b_out.partition_broadcast(P)).then_inc(w_att, 16)
                place_e(sp, 0, 0)
                sp.dma_start(wf_sb[:], w_ffn.rearrange("(k p) n -> p k n", p=P)).then_inc(w_ffn_in, 16)
                with nc.allow_non_contiguous_dma(reason="256 values"):
                    sp.dma_start(gam[:], ln_gamma.rearrange("(k p) -> p k", p=P)).then_inc(w_ffn_in, 16)
                    sp.dma_start(bet[:], ln_beta.rearrange("(k p) -> p k", p=P)).then_inc(w_ffn_in, 16)
                iterations(sp, sp_iteration)

                with sp.Fori(0, ST // 2) as i:
                    for b in range(2):
                        s = i * 2 + b
                        sp.wait_ge(y_ev, s * 3 + 3)
                        sp.dma_start(out[bass.ds(s, 1)].rearrange("s p f -> p s f"),
                                     H[:, bass.ds(s, 1), :]).then_inc(st_o[b], 16)
                for b in range(2):
                    sp.wait_ge(st_o[b], 16 * (ST // 2))


def kernel(x, txt, L0_tok_W, L0_tok_b, L0_tok_pos_emb, L0_attn_W_qkv, L0_attn_b_qkv, L0_attn_W_out, L0_attn_b_out,
           L0_ffn_weight, L0_ffn_ln_gamma, L0_ffn_ln_beta):
    import numpy as np
    import concourse.bacc as bacc
    from concourse.bass_utils import run_bass_kernel_spmd

    p = np.ascontiguousarray(x).reshape(ST, 8, 3, 4, 16, 4, 16).transpose(2, 4, 6, 0, 3, 5, 1)
    p = p.reshape(KX, P, ST, 16, 8)
    order = [n for r in range(R) for n in range(r, 16, R)]
    p = np.ascontiguousarray(p[:, :, :, order].transpose(2, 1, 0, 3, 4)).reshape(ST, P, KX * P)
    t = np.ascontiguousarray(txt).reshape(ST, 8, 32 * E)
    whole = np.ascontiguousarray(t[:, :, 2 * E:].reshape(ST, 8, 10, R * E).transpose(0, 2, 1, 3)).reshape(ST, 80, R * E)
    part = np.ascontiguousarray(t[:, :, 0:2 * E])
    arrays = {
        "x_patches": p, "txt_whole": whole, "txt_part": part, "tok_w": np.ascontiguousarray(np.transpose(L0_tok_W)),
        "tok_b": L0_tok_b, "pos": L0_tok_pos_emb, "w_qkv": L0_attn_W_qkv, "b_qkv": L0_attn_b_qkv,
        "w_out": L0_attn_W_out, "b_out": L0_attn_b_out, "w_ffn": L0_ffn_weight, "ln_gamma": L0_ffn_ln_gamma,
        "ln_beta": L0_ffn_ln_beta,
    }
    arrays = {n: np.ascontiguousarray(a) for n, a in arrays.items()}
    nc = bacc.Bacc("TRN2", target_bir_lowering=False, num_devices=1)
    args = [nc.dram_tensor(n, a.shape, mybir.dt.from_np(a.dtype), kind="ExternalInput").ap() for n, a in arrays.items()]
    args.append(nc.dram_tensor("out", (ST, P, R * E), F32, kind="ExternalOutput").ap())
    build(nc, *args)
    got = run_bass_kernel_spmd(nc, [arrays], core_ids=[0]).results[0]["out"]
    return np.ascontiguousarray(np.reshape(got, (ST, 16, 8, R * E)).transpose(0, 2, 1, 3)).reshape(128, 48, E)
```

```python
from contextlib import ExitStack

import concourse.bass as bass
from concourse import mybir

F32 = mybir.dt.float32
F16 = mybir.dt.float16
ALU = mybir.AluOpType
ACT = mybir.ActivationFunctionType
AX = mybir.AxisListType

P = 128
ST = 16
R = 3
J = 16
D = 16
S = R * J
SP2 = 64
E = 256
QKV = 3 * E
KT = E // P
KX = 768 // P
UNITS = 8
SLOTS = 8
SCALE = float(2 * E) ** -0.5
MASKED = -3.0e38
LN_EPS = 1e-5
FFN_LN_EPS = 1e-3
QB = 128.0
BOUND = float(E)
F16_TOP = 2.0 ** 15
TINY = 1e-30
CLIP = QB - 1e-5


def build(nc, x_patches, txt_whole, txt_part, tok_w, tok_b, pos, w_qkv, b_qkv, w_out, b_out, w_ffn,
          ln_gamma, ln_beta, out):
    with ExitStack() as ctx:
        def sb(name, shape, dt=F32):
            return ctx.enter_context(nc.sbuf_tensor(name, shape, dt))

        def sem(name):
            return ctx.enter_context(nc.semaphore(name))

        H = sb("H", [P, ST, R * E])
        XNT = sb("XNT", [P, ST, KT * R * P])
        wq16 = sb("wq16", [P, 2, KT, QKV], F16)
        wo_sb = sb("wo_sb", [P, KT, E])
        wf_sb = sb("wf_sb", [P, KT, E])
        tw_sb = sb("tw_sb", [P, KX, E])
        bq_sb = sb("bq_sb", [P, QKV])
        bo_sb = sb("bo_sb", [P, E])
        posb = sb("posb", [P, E])
        gam = sb("gam", [P, KT])
        bet = sb("bet", [P, KT])
        mask = sb("mask", [P, S])
        ident = sb("ident", [P, P])
        pmax = sb("pmax", [P, ST])
        small = sb("small", [P, 48])
        half = small[:, 27:30]
        xp = [sb(f"xp{i}", [P, KX, P]) for i in range(2)]
        emb = [sb(f"emb{i}", [P, E]) for i in range(2)]
        st1 = sb("st1", [P, R, 6])
        mv1 = sb("mv1", [P, R, 2])
        ve1 = small[:, 30:33]
        rs1 = small[:, 33:36]
        z1 = sb("z1", [P, R, E])
        hT = sb("hT", [P, KT, R * P])
        qkv = sb("qkv", [P, R, QKV])
        qp = [sb(f"qp{i}", [P, J, 32]) for i in range(2)]
        kp = [sb(f"kp{i}", [P, J, 32]) for i in range(2)]
        qT = [sb(f"qT{i}", [P, 32 * S]) for i in range(2)]
        kT = [sb(f"kT{i}", [P, 32 * S]) for i in range(2)]
        vT = [sb(f"vT{i}", [P, 64, D + 1]) for i in range(2)]
        Sm = [sb(f"Sm{i}", [P, SLOTS, S]) for i in range(2)]
        mx = [sb(f"mx{i}", [P, SLOTS]) for i in range(2)]
        Pr = [sb(f"Pr{i}", [P, SLOTS, SP2]) for i in range(2)]
        PT = [sb(f"PT{i}", [P, 4, P]) for i in range(2)]
        OT = sb("OT", [P, 32, S])
        O = sb("O", [P, S, 32])
        rc = O[:, :, D + 1]
        sa = z1
        st2 = sb("st2", [P, R, 6])
        mv2 = sb("mv2", [P, R, 2])
        ve2 = small[:, 36:39]
        rs2 = small[:, 39:42]
        z2 = sb("z2", [P, R, E])
        saT = z2[:].rearrange("p r e -> p (r e)").rearrange("p (k m) -> p k m", k=KT)
        zero = z2[:, 0, 0:P]
        wq_in = O[:].rearrange("p s g -> p (s g)")
        hT16 = hT[:].rearrange("p k n -> p (k n)").bitcast(F16).rearrange("p (w k n) -> p w k n", w=2, k=KT)

        def halves(t):
            h = t[:].bitcast(F16)
            return h.rearrange("p (c w) -> p c w", w=2) if len(h.shape) == 2 else h.rearrange("p j (c w) -> p j c w", w=2)

        qp16s, kp16s = [halves(t) for t in qp], [halves(t) for t in kp]
        qT16, kT16 = [halves(t) for t in qT], [halves(t) for t in kT]
        unscale = small[:, 22:23]

        psS = [ctx.enter_context(nc.psum_tensor(f"psS{i}", [P, SLOTS, SP2], F32)) for i in range(2)]
        psO = [ctx.enter_context(nc.psum_tensor(f"psO{i}", [P, 512], F32)) for i in range(2)]
        psP = ctx.enter_context(nc.psum_tensor("psP", [P, 4, P], F32))
        psA = [ctx.enter_context(nc.psum_tensor(f"psA{i}", [P, 512], F32)) for i in range(2)]
        psC = ctx.enter_context(nc.psum_tensor("psC", [P, 512], F32))

        w_tok, w_pos, w_q, w_o, w_ffn_in = sem("w_tok"), sem("w_pos"), sem("w_q"), sem("w_o"), sem("w_ffn_in")
        wq_max, wq_all, wq_sc = sem("wq_max"), sem("wq_all"), sem("wq_sc")
        wq_hi, wq_lo = sem("wq_hi"), sem("wq_lo")
        s_pos, s_abs = sem("s_pos"), sem("s_abs")
        s_zero, s_one, s_const, s_prep, s_pool0 = sem("s_zero"), sem("s_one"), sem("s_const"), sem("s_prep"), sem("s_pool0")
        ld_x = [sem(f"ld_x{i}") for i in range(2)]
        ld_t = [sem(f"ld_t{i}") for i in range(2)]
        ld_e = [sem(f"ld_e{i}") for i in range(2)]
        e_mm, e_ev = sem("e_mm"), sem("e_ev")
        bn1, av1, pw1, r1, zz1 = sem("bn1"), sem("av1"), sem("pw1"), sem("r1"), sem("zz1")
        h_mm, h_hi, h_ev = sem("h_mm"), sem("h_hi"), sem("h_ev")
        q_mm, q_ev, qk_hi, qk_lo, qk_t = sem("q_mm"), sem("q_ev"), sem("qk_hi"), sem("qk_lo"), sem("qk_t")
        v_mm, v_ev = sem("v_mm"), sem("v_ev")
        s_mm, s_ev, s_max, s_sub, s_exp = sem("s_mm"), sem("s_ev"), sem("s_max"), sem("s_sub"), sem("s_exp")
        p_mm, p_ev, o_mm, o_ev = sem("p_mm"), sem("p_ev"), sem("o_mm"), sem("o_ev")
        o_t, o_rc, o_sa = sem("o_t"), sem("o_rc"), sem("o_sa")
        c_mm, c_ev, w_mm, w_ev, h_bias = sem("c_mm"), sem("c_ev"), sem("w_mm"), sem("w_ev"), sem("h_bias")
        bn2, av2, pw2, r2, zz2 = sem("bn2"), sem("av2"), sem("pw2"), sem("r2"), sem("zz2")
        t_mm, t_ev, a_max = sem("t_mm"), sem("t_ev"), sem("a_max")
        g_max, g_all, g_sc = sem("g_max"), sem("g_all"), sem("g_sc")
        x_sc, x_cl, x_hi, x_lo = sem("x_sc"), sem("x_cl"), sem("x_hi"), sem("x_lo")
        y_mm, y_ev = sem("y_mm"), sem("y_ev")
        st_o = [sem(f"st_o{i}") for i in range(2)]

        ONES = 12

        def after(s, per, k):
            return s * per + k

        def alone(eng):
            eng.nop(nofuse=True)

        def A_bank(par, use):
            return psA[(par + use) % 2]

        def A_free(eng, s, use, emb=True):
            if use < 2 or (use == 2 and not emb):
                if not (isinstance(s, int) and s == 0):
                    eng.wait_ge(v_ev, after(s - 1, 4, 3 + use % 2))
            elif use == 2:
                eng.wait_ge(e_ev, after(s + 1, 1, 1))
            elif use < 5:
                eng.wait_ge(h_ev, after(s, 2, use - 2))
            elif use < 11:
                eng.wait_ge(q_ev, after(s, 6, use - 4))
            else:
                eng.wait_ge(v_ev, after(s, 4, use - 10))

        def unit(s, par, n, prev, cur):
            if n >= 0:
                return (s, par, n) if cur else None
            return (s - 1, 1 - par, n + UNITS) if prev else None

        def half_count(s, n):
            return s * 2 + n // 4

        def last(s):
            return isinstance(s, int) and s >= ST - 2

        def C_bank(s, use):
            return (psC, psA[0], psA[1])[use % 3] if last(s) else psC

        def pe_iteration(pe, s, par, prev, cur, nxt, emb):
            for t in range(8):
                pe_stages(pe, s, par, prev, nxt, emb, t, -1)
                if cur:
                    pe_scores(pe, s, par, t, 0, prev)
                pe_stages(pe, s, par, prev, nxt, emb, t, 0)
                if cur:
                    pe_scores(pe, s, par, t, 1, prev)
                pe_stages(pe, s, par, prev, nxt, emb, t, 1)
                if u := unit(s, par, t - 2, prev, cur):
                    pe_values(pe, *u)
                pe_stages(pe, s, par, prev, nxt, emb, t, 2)
                if u := unit(s, par, t - 1, prev, cur):
                    pe_turn(pe, *u)
                pe_stages(pe, s, par, prev, nxt, emb, t, 3)

        def pe_scores(pe, s, par, t, part, prev):
            c, hh = t % 4, t // 4
            if part == 0:
                if t == 0:
                    pe.wait_ge(qk_t, after(s, 6, 6))
                if t >= 2 or prev:
                    pe.wait_ge(s_ev, after(s, 8, t - 1))
                alone(pe)
            for slot in range(4 * part, 4 * part + 4):
                for v in range(2):
                    g = 16 * hh + 2 * slot + v
                    for low in range(2):
                        mm = nc.tensor.matmul(psS[t % 2][64 * v:64 * v + S, slot, 0:S],
                                              qT16[par][32 * c:32 * c + 32, g * S:(g + 1) * S, 1],
                                              kT16[par][32 * c:32 * c + 32, g * S:(g + 1) * S, 1 - low],
                                              start=(low == 0), stop=(low == 1))
            if part == 1:
                mm.then_inc(s_mm, 1)

        def pe_turn(pe, us, up, un):
            pe.wait_ge(s_exp, after(us, 8, un + 1))
            if un > 0 or not (isinstance(us, int) and us == 0):
                pe.wait_ge(p_ev, after(us, 8, un))
            for k in range(4):
                mm = nc.tensor.transpose(psP[:, k, :], Pr[un % 2][:, 2 * k:2 * k + 2, :].rearrange("p a b -> p (a b)"),
                                         ident[:])
            mm.then_inc(p_mm, 1)

        def pe_values(pe, us, up, un):
            c, hh = un % 4, un // 4
            pe.wait_ge(p_ev, after(us, 8, un + 1))
            if un == 0:
                pe.wait_ge(v_ev, after(us, 4, 4))
            if c == 0 and not (isinstance(us, int) and us == 0 and hh == 0):
                pe.wait_ge(o_ev, half_count(us, un))
            alone(pe)
            for hu in range(2):
                for kk in range(4):
                    for v in range(2):
                        g = c * 16 + (4 * hh + kk) * 2 + v
                        mm = nc.tensor.matmul(psO[hu][32 * c:32 * c + D + 1, (2 * kk + v) * S:(2 * kk + v + 1) * S],
                                              vT[up][64 * hu:64 * hu + S, g, :],
                                              PT[un % 2][64 * hu:64 * hu + S, kk, 64 * v:64 * v + S],
                                              start=True, stop=True)
            mm.then_inc(o_mm, 1)

        EMBED = [(0, -1), (0, 1)]
        NORM = (1, 1)
        PROJECT = [(1, 3), (2, 1), (2, 2), (3, 0), (4, 1), (5, 1)]
        VALUES = [(6, 1), (6, 3)]
        OUTPUTS = [(2, 3), (3, 1)]
        PROJECT_OUT = [(3, 3), (4, 2), (5, 0)]
        NORM2 = [(7, 1), (7, 3)]

        def pe_stages(pe, s, par, prev, nxt, emb, t, part):
            at = (t, part)
            n, p = s + 1, 1 - par
            if emb and at in EMBED:
                pe_embed(pe, s + 2, par, EMBED.index(at))
            if nxt and at == NORM:
                pe_norm(pe, n, p, emb)
            if prev and at in OUTPUTS:
                pe_turn_outputs(pe, s - 1, OUTPUTS.index(at))
            if nxt and at in PROJECT:
                pe_project(pe, n, p, PROJECT.index(at) // 2, PROJECT.index(at) % 2)
            if nxt and at in VALUES:
                pe_turn_values(pe, n, p, VALUES.index(at))
            if prev and at in PROJECT_OUT:
                pe_project_out(pe, s - 1, PROJECT_OUT.index(at))
            if prev and at in NORM2:
                pe_turn_norm(pe, s - 1, NORM2.index(at))

        def pe_embed(pe, s, par, part):
            if part == 0:
                pe.wait_ge(ld_x[par], (s - par) * 8 + 16)
                if not (isinstance(s, int) and s == 0):
                    A_free(pe, s - 1, 0)
            for k in range(part * KX // 2, (part + 1) * KX // 2):
                mm = nc.tensor.matmul(A_bank(1 - par, 0)[:, 0:E], xp[par][:, k, :], tw_sb[:, k, :],
                                      start=(k == 0), stop=(k == KX - 1))
            if part == 1:
                mm.then_inc(e_mm, 1)

        def pe_norm(pe, s, par, emb):
            pe.wait_ge(zz1, after(s, 3, 3))
            for k in range(KT):
                A_free(pe, s, 1 + k, emb)
                for r in range(R):
                    mm = nc.tensor.transpose(A_bank(par, 1 + k)[:, r * P:(r + 1) * P], z1[:, r, k * P:(k + 1) * P],
                                             ident[:])
                mm.then_inc(h_mm, 1)

        def pe_project(pe, s, par, r, ch):
            if (r, ch) == (0, 0):
                pe.wait_ge(h_ev, after(s, 2, 2))
                if isinstance(s, int) and s == 0:
                    pe.wait_ge(wq_lo, 1)
            A_free(pe, s, 3 + 2 * r + ch)
            for i, (hw, ww) in enumerate(((0, 0), (1, 0), (0, 1))):
                for k in range(KT):
                    mm = nc.tensor.matmul(A_bank(par, 3 + 2 * r + ch)[:, 0:384], hT16[:, hw, k, r * P:(r + 1) * P],
                                          wq16[:, ww, k, ch * 384:(ch + 1) * 384], start=(i == 0 and k == 0),
                                          stop=(i == 2 and k == KT - 1))
            mm.then_inc(q_mm, 1)

        def pe_turn_values(pe, s, par, part):
            if part == 0:
                pe.wait_ge(q_ev, after(s, 6, 6))
            rows = qkv[:].rearrange("p r (j c) -> p (r j) c", c=S)
            for q in range(2 * part, 2 * part + 2):
                A_free(pe, s, 9 + q)
                alone(pe)
                for i in range(4):
                    mm = nc.tensor.transpose(A_bank(par, 9 + q)[0:S, i * P:(i + 1) * P], rows[:, :, 2 * D + 4 * q + i],
                                             ident[:])
                mm.then_inc(v_mm, 1)

        def pe_turn_outputs(pe, s, k):
            if k == 0:
                pe.wait_ge(o_sa, after(s, 1, 1))
                if not (isinstance(s, int) and s == 0):
                    pe.wait_ge(t_ev, after(s - 1, 2, 2))
                if last(s):
                    pe.wait_ge(v_ev, 4 * ST)
            elif not last(s):
                pe.wait_ge(c_ev, after(s, 2, 1))
            for r in range(R):
                mm = nc.tensor.transpose(C_bank(s, k)[:, r * P:(r + 1) * P], sa[:, r, k * P:(k + 1) * P], ident[:])
            mm.then_inc(c_mm, 1)

        def pe_project_out(pe, s, r):
            if r == 0:
                pe.wait_ge(c_ev, after(s, 2, 2))
            elif not last(s):
                pe.wait_ge(w_ev, after(s, 3, r))
            for k in range(KT):
                mm = nc.tensor.matmul(C_bank(s, 2 + r)[:, 0:E], saT[:, k, r * P:(r + 1) * P], wo_sb[:, k, :],
                                      start=(k == 0), stop=(k == KT - 1))
            mm.then_inc(w_mm, 1)

        def pe_turn_norm(pe, s, k):
            if k == 0:
                pe.wait_ge(zz2, after(s, 3, 3))
                pe.wait_ge(w_ev, after(s, 3, 3))
            elif not last(s):
                pe.wait_ge(t_ev, after(s, 2, 1))
            for r in range(R):
                mm = nc.tensor.transpose(C_bank(s, 5 + k)[:, r * P:(r + 1) * P], z2[:, r, k * P:(k + 1) * P], ident[:])
            mm.then_inc(t_mm, 1)

        def act_iteration(act, s, par, prev, cur, nxt, emb):
            n, p = s + 1, 1 - par
            for t in range(8):
                if nxt and t == 1:
                    act_norm1(act, n, p)
                if (u := unit(s, par, t - 2, prev, cur)) and u[2] % 4 == 3:
                    act_half(act, *u)
                if prev and t == 3:
                    act_outputs(act, s - 1, 1)
                if prev and t == 7:
                    act_norm2(act, s - 1, 0)
                if nxt and t == 7:
                    act_values(act, n, p, 1)
                if nxt and t == 4:
                    act_high(act, n, 1)
                if u := unit(s, par, t - 1, prev, cur):
                    us, up, un = u
                    act.wait_ge(p_mm, after(us, 8, un + 1))
                    if un >= 2 or not (isinstance(us, int) and us == 0):
                        act.wait_ge(o_mm, after(us, 8, un - 1))
                    nc.scalar.activation(PT[un % 2][:], psP[:], ACT.Copy).then_inc(p_ev, 1)
                if prev and t == 7:
                    act_norm2(act, s - 1, 1)
                if cur:
                    act.wait_ge(s_sub, after(s, 8, t + 1))
                    nc.scalar.activation(Pr[t % 2][:, :, 0:S], Pr[t % 2][:, :, 0:S], ACT.Exp).then_inc(s_exp, 1)
                if prev and t == 2:
                    act_outputs(act, s - 1, 0)
                if nxt and t == 2:
                    act_high(act, n, 0)
                if nxt and t == 5:
                    if not cur:
                        act_high(act, n, 2)
                    act_values(act, n, p, 0)
                    if cur:
                        act_high(act, n, 2)

        def act_high(act, s, r):
            act.wait_ge(q_ev, after(s, 6, 2 * r + 2))
            if r == 2:
                act.wait_ge(qk_t, after(s, 6, 2))
            elif not (isinstance(s, int) and s == 0):
                act.wait_ge(qk_t, after(s - 1, 6, 4 if r else 6))
            qp16, kp16 = qp16s[r % 2], kp16s[r % 2]
            rows = qkv[:, r, :].rearrange("p (j c) -> p j c", c=S)
            nc.scalar.activation(qp16[:, :, 0:D, 1], rows[:, :, 0:D], ACT.Copy).then_inc(qk_hi, 1)
            nc.scalar.activation(kp16[:, :, :, 1].rearrange("p j (u d) -> p j u d", u=2),
                                 rows[:, :, D:2 * D].unsqueeze(2).to_broadcast([P, J, 2, D]), ACT.Copy).then_inc(qk_hi, 1)

        def act_norm1(act, s, par):
            if not (isinstance(s, int) and s == 0):
                act.wait_ge(q_mm, after(s - 1, 6, 6))
            for k in range(KT):
                act.wait_ge(h_mm, after(s, 2, k + 1))
                nc.scalar.activation(hT16[:, 0, k, :], A_bank(par, 1 + k)[:, 0:R * P], ACT.Copy).then_inc(h_hi, 1)

        def act_values(act, s, par, part):
            if part == 0 and not (isinstance(s, int) and s < 2):
                act.wait_ge(o_mm, after(s - 2, 8, 8))
            for q in range(2 * part, 2 * part + 2):
                act.wait_ge(v_mm, after(s, 4, q + 1))
                src = A_bank(par, 9 + q)[0:S, :].rearrange("p (e g u v) -> p u g v e", e=4, u=2, v=2)
                for hu in range(2):
                    dst = vT[par][64 * hu:64 * hu + S, :, 4 * q:4 * q + 4].rearrange("p (g v) e -> p g v e", v=2)
                    a = nc.scalar.activation(dst, src[:, hu], ACT.Copy)
                a.then_inc(v_ev, 1)

        def act_half(act, us, up, un):
            hh = un // 4
            act.wait_ge(o_mm, after(us, 8, un + 1))
            if hh == 0 and not (isinstance(us, int) and us == 0):
                act.wait_ge(o_t, after(us - 1, 1, 1))
            for hu in range(2):
                dst = OT[:, 16 * hh:16 * hh + 16, :].rearrange("p (k u v) s -> p u k v s", u=2, v=2)[:, hu]
                src = psO[hu][:, 0:8 * S].rearrange("p (k v s) -> p k v s", k=4, v=2)
                a = nc.scalar.activation(dst, src, ACT.Copy)
            a.then_inc(o_ev, 1)

        def act_outputs(act, s, k):
            if k == 0 and not (isinstance(s, int) and s == 0):
                act.wait_ge(t_mm, after(s - 1, 2, 2))
            act.wait_ge(c_mm, after(s, 2, k + 1))
            nc.scalar.activation(saT[:, k, :], C_bank(s, k)[:, 0:R * P], ACT.Copy).then_inc(c_ev, 1)

        def act_norm2(act, s, k):
            act.wait_ge(t_mm, after(s, 2, k + 1))
            dst = XNT[:, bass.ds(s, 1), k * R * P:(k + 1) * R * P]
            nc.scalar.activation(dst, C_bank(s, 5 + k)[:, 0:R * P].unsqueeze(1), ACT.Identity, bias=bet[:, k:k + 1],
                                 scale=gam[:, k:k + 1]).then_inc(t_ev, 1)

        def pool_iteration(pool, s, par, prev, cur, nxt, emb):
            for t in range(8):
                if cur:
                    pool.wait_ge(s_max, after(s, 8, t + 1))
                    if t >= 2 or prev:
                        pool.wait_ge(p_mm, after(s, 8, t - 1))
                    nc.gpsimd.tensor_tensor(Pr[t % 2][:, :, 0:S], Sm[t % 2][:],
                                            mx[t % 2][:].unsqueeze(2).to_broadcast([P, SLOTS, S]),
                                            ALU.subtract).then_inc(s_sub, 1)
                if nxt and t == 2:
                    pool.wait_ge(zz1, after(s + 1, 3, 3))
                    h = H[:, bass.ds(s + 1, 1), :].rearrange("p a (r e) -> p (a r) e", r=R)
                    nc.gpsimd.tensor_tensor(h, h, bo_sb[:].unsqueeze(1).to_broadcast([P, R, E]),
                                            ALU.add).then_inc(h_bias, 1)
                if prev and t == 5:
                    power(pool, s - 1, av2, mv2, ve2, 1.0 + FFN_LN_EPS, FFN_LN_EPS * LN_EPS, pw2, zz2, rs2, r2)

                if nxt and t in (3, 4, 6):
                    pool_low(pool, s + 1, (3, 4, 6).index(t))
                if emb and t == 4:
                    power1(pool, s + 2)

        def pool_low(pool, s, r):
            qp16, kp16 = qp16s[r % 2], kp16s[r % 2]
            rows = qkv[:, r, :].rearrange("p (j c) -> p j c", c=S)
            pool.wait_ge(qk_hi, after(s, 6, 2 * r + 2))
            nc.gpsimd.tensor_tensor(qp16[:, :, D:2 * D, 1], rows[:, :, 0:D], qp16[:, :, 0:D, 1],
                                    ALU.subtract).then_inc(qk_lo, 1)
            nc.gpsimd.tensor_tensor(kp16[:, :, :, 0].rearrange("p j (u d) -> p j u d", u=2),
                                    rows[:, :, D:2 * D].unsqueeze(2).to_broadcast([P, J, 2, D]),
                                    kp16[:, :, :, 1].rearrange("p j (u d) -> p j u d", u=2),
                                    ALU.subtract).then_inc(qk_lo, 1)

        def power1(pool, s):
            power(pool, s, av1, mv1, ve1, 1.0, LN_EPS, pw1, zz1, rs1, r1)

        def power(pool, s, av, mv, ve, a, b, done, used, rs, ready):
            pool.wait_ge(av, after(s, 3, 3))
            alone(pool)
            nc.gpsimd.tensor_scalar(ve, mv[:, :, 1], a, b, ALU.mult, ALU.add).then_inc(done, 1)
            pool.wait_ge(done, after(s, 1, 1))
            if not (isinstance(s, int) and s == 0):
                pool.wait_ge(used, after(s - 1, 3, 3))
            nc.gpsimd.tensor_tensor(rs, ve, half, ALU.pow).then_inc(ready, 1)

        def dve_iteration(dve, s, par, prev, cur, nxt, emb):
            n, p = s + 1, 1 - par
            for t in range(8):
                if cur:
                    dve.wait_ge(s_mm, after(s, 8, t + 1))
                    if t >= 2 or prev:
                        dve.wait_ge(s_sub, after(s, 8, t - 1))
                    nc.vector.scalar_tensor_tensor(Sm[t % 2][:], psS[t % 2][:, :, 0:S], unscale,
                                                   mask[:].unsqueeze(1).to_broadcast([P, SLOTS, S]),
                                                   ALU.mult, ALU.add).then_inc(s_ev, 1)
                    dve.wait_ge(s_ev, after(s, 8, t + 1))
                    nc.vector.tensor_reduce(mx[t % 2][:], Sm[t % 2][:], AX.X, ALU.max).then_inc(s_max, 1)
                if nxt and t == 0:
                    dve.wait_ge(r1, after(n, 1, 1))
                    if not (isinstance(s, int) and s == -1):
                        dve.wait_ge(h_mm, after(s, 2, 2))
                    for r in range(R):
                        nc.vector.tensor_scalar(z1[:, r, :].unsqueeze(1), H[:, bass.ds(n, 1), r * E:(r + 1) * E], mv1[:, r, 0:1],
                                                rs1[:, r:r + 1], ALU.subtract, ALU.mult).then_inc(zz1, 1)
                if emb and t == 0:
                    dve_embed(dve, s + 2, par)
                if nxt and t == 1:
                    for k in range(KT):
                        dve.wait_ge(h_hi, after(n, 2, k + 1))
                        nc.vector.tensor_tensor(hT16[:, 1, k, :], A_bank(p, 1 + k)[:, 0:R * P], hT16[:, 0, k, :],
                                                ALU.subtract).then_inc(h_ev, 1)
                if prev and t == 1:
                    dve.wait_ge(o_ev, after(s - 1, 2, 2))
                    nc.vector.transpose(O[:], OT[:].rearrange("p g s -> p s g")).then_inc(o_t, 1)
                    dve.wait_ge(o_t, after(s - 1, 1, 1))
                    nc.vector.reciprocal(rc, O[:, :, D]).then_inc(o_rc, 1)
                if nxt and t == 2:
                    dve_project(dve, n, p, 0, 0)
                if prev and t == 2:
                    dve.wait_ge(o_rc, after(s - 1, 1, 1))
                    if not (isinstance(s, int) and s == 1):
                        dve.wait_ge(c_mm, after(s - 2, 2, 2))
                    nc.vector.tensor_tensor(sa[:].rearrange("p r (j e) -> p (r j) e", e=D), O[:, :, 0:D],
                                            rc.unsqueeze(2).to_broadcast([P, S, D]), ALU.mult).then_inc(o_sa, 1)
                if nxt and t == 2:
                    dve_project(dve, n, p, 0, 1)
                if prev and t == 2 and not (isinstance(s, int) and s < 2):
                    dve_largest(dve, s - 2)
                if nxt and t == 3:
                    dve_project(dve, n, p, 1, 0)
                    dve_project(dve, n, p, 1, 1)
                if prev and t == 4:
                    dve_residual(dve, s - 1, 0)
                if nxt and t == 4:
                    dve_turn(dve, n, p, 0)
                if nxt and t == 4:
                    dve_project(dve, n, p, 2, 0)
                if prev and t == 4:
                    dve_residual(dve, s - 1, 1)
                if emb and t == 4:
                    stats1(dve, s + 2, par)
                if prev and t == 5:
                    dve_residual(dve, s - 1, 2)
                if nxt and t == 5:
                    dve_project(dve, n, p, 2, 1)
                if prev and t == 5:
                    dve.wait_ge(w_ev, after(s - 1, 3, 3))
                    stats(dve, s - 1, st2, mv2, bn2, av2)
                if nxt and t == 5:
                    dve_turn(dve, n, p, 1)
                if prev and t == 6:
                    dve.wait_ge(r2, after(s - 1, 1, 1))
                    if not (isinstance(s, int) and s == 1):
                        dve.wait_ge(t_mm, after(s - 2, 2, 2))
                    for r in range(R):
                        nc.vector.tensor_scalar(z2[:, r, :].unsqueeze(1), H[:, bass.ds(s - 1, 1), r * E:(r + 1) * E],
                                                mv2[:, r, 0:1], rs2[:, r:r + 1], ALU.subtract, ALU.mult).then_inc(zz2, 1)
                if nxt and t == 7:
                    dve_turn(dve, n, p, 2)

        def dve_largest(dve, s):
            dve.wait_ge(t_ev, after(s, 2, 2))
            nc.vector.tensor_reduce(pmax[:, bass.ds(s, 1)], XNT[:, bass.ds(s, 1), :], AX.X, ALU.max,
                                    apply_absolute_value=True).then_inc(a_max, 1)

        def stats1(dve, s, par):
            dve.wait_ge(ld_e[par], (s - par) * 24 + 48)
            dve.wait_ge(ld_t[par], (s - par) * 16 + 32)
            stats(dve, s, st1, mv1, bn1, av1)

        def dve_embed(dve, s, par):
            dve.wait_ge(e_mm, after(s, 1, 1))
            if not (isinstance(s, int) and s < 2):
                dve.wait_ge(ld_e[par], (s - par) * 24)
            nc.vector.tensor_tensor(emb[par][:], A_bank(1 - par, 0)[:, 0:E], posb[:], ALU.add).then_inc(e_ev, 1)

        def dve_residual(dve, s, r):
            dve.wait_ge(w_mm, after(s, 3, r + 1))
            if r == 0:
                dve.wait_ge(h_bias, after(s, 1, 1))
            h = H[:, bass.ds(s, 1), r * E:(r + 1) * E]
            nc.vector.tensor_tensor(h, h, C_bank(s, 2 + r)[:, 0:E].unsqueeze(1), ALU.add).then_inc(w_ev, 1)

        def dve_project(dve, s, par, r, ch):
            if (r, ch) == (0, 0) and not (isinstance(s, int) and s == 0):
                dve.wait_ge(v_mm, after(s - 1, 4, 4))
                dve.wait_ge(qk_lo, after(s - 1, 6, 6))
            dve.wait_ge(q_mm, after(s, 6, 2 * r + ch + 1))
            nc.vector.tensor_tensor(qkv[:, r, ch * 384:(ch + 1) * 384], A_bank(par, 3 + 2 * r + ch)[:, 0:384],
                                    bq_sb[:, ch * 384:(ch + 1) * 384], ALU.add).then_inc(q_ev, 1)

        def dve_turn(dve, s, par, r):
            if r == 0 and not (isinstance(s, int) and s < 2):
                dve.wait_ge(s_mm, after(s - 2, 8, 8))
            dve.wait_ge(qk_lo, after(s, 6, 2 * r + 2))
            for dst, src in ((qT[par], qp[r % 2]), (kT[par], kp[r % 2])):
                view = dst[:].rearrange("p (g s) -> p s g", s=S)[:, r * J:(r + 1) * J, :]
                nc.vector.transpose(view, src[:]).then_inc(qk_t, 1)

        def stats(dve, s, st, mv, bn, av):
            alone(dve)
            for r in range(R):
                nc.vector.bn_stats(st[:, r, :], H[:, bass.ds(s, 1), r * E:(r + 1) * E]).then_inc(bn, 1)
            dve.wait_ge(bn, after(s, 3, 3))
            alone(dve)
            for r in range(R):
                nc.vector.bn_aggr(mv[:, r, :], st[:, r, :]).then_inc(av, 1)

        def load_x(sp, s, par):
            if not (isinstance(s, int) and s < 2):
                sp.wait_ge(e_mm, after(s - 2, 1, 1))
            sp.dma_start(xp[par][:].rearrange("p k m -> p (k m)").unsqueeze(1),
                         x_patches[bass.ds(s, 1)].rearrange("s p f -> p s f")).then_inc(ld_x[par], 16)

        def load_t(sp, s, par):
            if not (isinstance(s, int) and s < 2):
                sp.wait_ge(ld_t[par], (s - par) * 16)
            sp.dma_start(H[48:P, bass.ds(s, 1), :], txt_whole[bass.ds(s, 1)].rearrange("s p f -> p s f")).then_inc(ld_t[par], 16)
            sp.dma_start(H[40:48, bass.ds(s, 1), E:3 * E], txt_part[bass.ds(s, 1)].rearrange("s p f -> p s f")).then_inc(ld_t[par], 16)

        def place_e(sp, s, par):
            sp.wait_ge(e_ev, after(s, 1, 1))
            for r, (a, b) in enumerate(((0, 48), (48, 88), (88, 128))):
                sp.dma_start(H[0:b - a, bass.ds(s, 1), r * E:(r + 1) * E], emb[par][a:b, :].unsqueeze(1)).then_inc(ld_e[par], 16)

        def sp_iteration(sp, s, par, loads_x=True):
            if loads_x:
                load_x(sp, s + 3, 1 - par)
            load_t(sp, s + 2, par)
            place_e(sp, s + 2, par)

        def iterations(eng, iteration, after_first=None):
            iteration(eng, -1, 1, False, False, True, True)
            if after_first:
                after_first()
            iteration(eng, 0, 0, False, True, True, True)
            iteration(eng, 1, 1, True, True, True, True)
            with eng.Fori(1, ST // 2 - 1) as i:
                iteration(eng, i * 2, 0, True, True, True, True)
                iteration(eng, i * 2 + 1, 1, True, True, True, True)
            iteration(eng, ST - 2, 0, True, True, True, False)
            iteration(eng, ST - 1, 1, True, True, False, False)
            iteration(eng, ST, 0, True, False, False, False)

        xs = [xp[i][:].rearrange("p k m -> p (k m)")[:, 0:KT * R * P] for i in range(2)]
        xq = [O[:].rearrange("p s g -> p (s g)")[:, i * KT * R * P:(i + 1) * KT * R * P] for i in range(2)]
        xhl = [z[:].rearrange("p r e -> p (r e)").bitcast(F16).rearrange("p (w n) -> p w n", w=2) for z in (z1, z2)]
        wt = qp[0][:].rearrange("p j c -> p (j c)").bitcast(F16)[:, 0:KT * E].rearrange("p (k n) -> p k n", k=KT)
        ybanks = [psS[0], psS[1], psP, psA[0], psA[1], psC]
        ybank = [b[:].rearrange("p a b -> p (a b)") if len(b[:].shape) == 3 else b[:] for b in ybanks]

        def quantised(eng, one):
            for b in range(2):
                one(b, b)
            with eng.Fori(1, ST // 2 - 1) as i:
                for b in range(2):
                    one(i * 2 + b, b)
            for b in range(2):
                one(ST - 2 + b, b)

        def first(s, n):
            return isinstance(s, int) and s < n

        with nc.Block() as block:
            @block.gpsimd
            def _(pool):
                nc.gpsimd.memset(zero, 0.0).then_inc(s_zero, 1)
                nc.gpsimd.memset(mask[:], 0.0).then_inc(s_zero, 1)
                pool.wait_ge(s_zero, 2)
                nc.gpsimd.affine_select(out=ident[:], in_=zero, compare_op=ALU.not_equal, fill=1.0, base=0,
                                        pattern=[[-1, P]], channel_multiplier=1).then_inc(s_const, 1)
                for v in range(2):
                    pool.wait_ge(s_const, v + 1)
                    m = mask[64 * v:64 * v + 64, :]
                    nc.gpsimd.affine_select(out=m, in_=m, compare_op=ALU.is_ge, fill=MASKED, base=0,
                                            pattern=[[-1, S]], channel_multiplier=1).then_inc(s_const, 1)

                def mean():
                    pool.wait_ge(s_abs, 1)
                    nc.gpsimd.partition_all_reduce(small[:, 1:2], small[:, 0:1], P,
                                                   bass.bass_isa.ReduceOp.add).then_inc(s_pool0, 1)

                pool.wait_ge(s_one, ONES)
                pool.wait_ge(s_const, 3)
                pool.wait_ge(wq_max, 4)
                nc.gpsimd.partition_all_reduce(small[:, 17:20], small[:, 11:14], P,
                                               bass.bass_isa.ReduceOp.max).then_inc(wq_all, 1)
                pool.wait_ge(wq_all, 1)
                pool.wait_ge(w_o, 16 * 2)
                power1(pool, 0)
                pool.wait_ge(wq_hi, 1)
                flat16 = wq16[:].rearrange("p w k n -> p w (k n)")
                nc.gpsimd.tensor_tensor(flat16[:, 1, :], wq_in, flat16[:, 0, :], ALU.subtract).then_inc(wq_lo, 1)
                iterations(pool, pool_iteration, mean)
                pool.wait_ge(g_max, 1)
                nc.gpsimd.partition_all_reduce(small[:, 6:7], small[:, 5:6], P, bass.bass_isa.ReduceOp.max).then_inc(g_all, 1)
                pool.wait_ge(g_all, 1)

                def pool_low2(s, b):
                    pool.wait_ge(x_hi, s + 1)
                    nc.gpsimd.tensor_tensor(xhl[b][:, 1, :], xq[b], xhl[b][:, 0, :], ALU.subtract).then_inc(x_lo, 1)

                quantised(pool, pool_low2)

            @block.scalar
            def _(act):
                act.wait_ge(s_one, ONES)
                nc.scalar.activation(small[:, 26:27], small[:, 9:10], ACT.Exp)
                act.wait_ge(wq_sc, 7)
                nc.scalar.activation(wq16[:].rearrange("p w k n -> p w (k n)")[:, 0, :], wq_in, ACT.Copy).then_inc(wq_hi, 1)
                act.wait_ge(w_ffn_in, 16 * 3)
                iterations(act, act_iteration)
                act.wait_ge(g_sc, 3)

                def act_scale(s, b):
                    if not first(s, 2):
                        act.wait_ge(x_cl, s - 1)
                    nc.scalar.activation(xs[b].unsqueeze(1), XNT[:, bass.ds(s, 1), :], ACT.Identity, bias=small[:, 9:10],
                                         scale=small[:, 10:11]).then_inc(x_sc, 1)

                def act_high2(s, b):
                    if not (isinstance(s, int) and s == ST - 1):
                        act_scale(s + 1, 1 - b)
                    act.wait_ge(x_cl, s + 1)
                    if not first(s, 2):
                        act.wait_ge(y_mm, s * 3 - 3)
                    nc.scalar.activation(xhl[b][:, 0, :], xq[b], ACT.Copy).then_inc(x_hi, 1)

                act_scale(0, 0)
                quantised(act, act_high2)

            @block.vector
            def _(dve):
                for b in range(2):
                    nc.vector.memset(psS[b][:], 0.0).then_inc(s_one, 1)
                    nc.vector.memset(Pr[b][:], 0.0).then_inc(s_one, 1)
                    nc.vector.memset(vT[b][:, :, D:D + 1], 1.0).then_inc(s_one, 1)
                    nc.vector.memset(psO[b][:], 0.0).then_inc(s_one, 1)
                    nc.vector.memset(qp[b][:], 0.0).then_inc(s_one, 1)
                nc.vector.memset(half, -0.5).then_inc(s_one, 1)
                nc.vector.memset(small[:, 9:10], 0.0).then_inc(s_one, 1)
                dve.wait_ge(w_pos, 16 * 4)
                nc.vector.tensor_tensor(posb[:], posb[:], emb[1][:], ALU.add).then_inc(s_pos, 1)
                dve.wait_ge(s_pos, 1)
                dve_embed(dve, 0, 0)

                dve.wait_ge(w_q, 16 * 2)
                wq_parts = wq_in.rearrange("p (a g d) -> p a g d", g=3, d=D)
                bq_parts = bq_sb[:].rearrange("p (a g d) -> p a g d", g=3, d=D)
                for i, (parts, largest) in enumerate(((wq_parts, small[:, 11:14]), (bq_parts, small[:, 14:17]))):
                    rows = OT[:].rearrange("p g s -> p (g s)")[:, 0:parts.shape[1] * 3].rearrange("p (a g) -> p a g", g=3)
                    nc.vector.tensor_reduce(rows, parts, AX.X, ALU.max, apply_absolute_value=True).then_inc(wq_max, 1)
                    dve.wait_ge(wq_max, 2 * i + 1)
                    nc.vector.tensor_reduce(largest, rows.rearrange("p a g -> p g a"), AX.X, ALU.max).then_inc(wq_max, 1)
                    dve.wait_ge(wq_max, 2 * i + 2)
                stats1(dve, 0, 0)
                bound, inverse, scale = small[:, 23:26], small[:, 42:45], small[:, 45:48]
                dve.wait_ge(wq_all, 1)
                nc.vector.scalar_tensor_tensor(bound, small[:, 17:20], BOUND, small[:, 14:17], ALU.mult,
                                               ALU.add).then_inc(wq_sc, 1)
                dve.wait_ge(wq_sc, 1)
                nc.vector.tensor_scalar(inverse, bound, 1.0 / F16_TOP, TINY, ALU.mult, ALU.add).then_inc(wq_sc, 1)
                dve.wait_ge(wq_sc, 2)
                nc.vector.reciprocal(scale, inverse).then_inc(wq_sc, 1)
                nc.vector.scalar_tensor_tensor(unscale, inverse[:, 0:1], SCALE, inverse[:, 1:2], ALU.mult,
                                               ALU.mult).then_inc(wq_sc, 1)
                dve.wait_ge(wq_sc, 4)
                for g in range(3):
                    nc.vector.tensor_scalar(wq_parts[:, :, g, :], wq_parts[:, :, g, :], scale[:, g:g + 1], None,
                                            ALU.mult).then_inc(wq_sc, 1)
                for g in range(3):
                    nc.vector.tensor_scalar(bq_parts[:, :, g, :], bq_parts[:, :, g, :], scale[:, g:g + 1], None,
                                            ALU.mult).then_inc(wq_sc, 1)
                dve.wait_ge(s_one, ONES)
                for b in range(2):
                    ones = vT[b][:, :, D:D + 1]
                    nc.vector.tensor_scalar(ones, ones, scale[:, 2:3], None, ALU.mult).then_inc(wq_sc, 1)
                dve.wait_ge(wq_sc, 12)
                dve.wait_ge(s_const, 3)

                def weight_sum():
                    dve.wait_ge(w_ffn_in, 16 * 3)
                    nc.vector.tensor_reduce(small[:, 0:1], wf_sb[:].rearrange("p k n -> p (k n)"), AX.X, ALU.add,
                                            apply_absolute_value=True).then_inc(s_abs, 1)

                iterations(dve, dve_iteration, weight_sum)

                prep = [0]

                def step(ins):
                    prep[0] += 1
                    ins.then_inc(s_prep, 1)
                    dve.wait_ge(s_prep, prep[0])

                dve.wait_ge(s_pool0, 1)
                dve.wait_ge(q_mm, 6 * ST)
                step(nc.vector.tensor_scalar(small[:, 2:3], small[:, 1:2], 1.0 / (E * E), None, ALU.mult))
                step(nc.vector.tensor_scalar(small[:, 3:4], small[:, 2:3], 1e-5, 0.5, ALU.add, ALU.mult))
                step(nc.vector.tensor_scalar(small[:, 4:5], small[:, 3:4], -1.0, None, ALU.mult))
                flat = wf_sb[:].rearrange("p k n -> p (k n)")
                below = hT[:].rearrange("p k n -> p (k n)")[:, 0:KT * E]
                step(nc.vector.tensor_scalar(below, flat, small[:, 4:5], None, ALU.is_lt))
                step(nc.vector.scalar_tensor_tensor(wt.rearrange("p k n -> p (k n)"), flat, small[:, 3:4], below, ALU.is_gt,
                                                    ALU.subtract))

                dve_largest(dve, ST - 1)
                dve.wait_ge(a_max, ST)
                nc.vector.tensor_reduce(small[:, 5:6], pmax[:], AX.X, ALU.max).then_inc(g_max, 1)
                dve.wait_ge(g_all, 1)
                nc.vector.reciprocal(small[:, 7:8], small[:, 6:7]).then_inc(g_sc, 1)
                nc.vector.tensor_scalar(small[:, 8:9], small[:, 6:7], small[:, 2:3], 1.0 / QB, ALU.mult,
                                        ALU.mult).then_inc(g_sc, 1)
                dve.wait_ge(g_sc, 2)
                nc.vector.tensor_scalar(small[:, 10:11], small[:, 7:8], QB, None, ALU.mult).then_inc(g_sc, 1)

                def dve_clip(s, b):
                    dve.wait_ge(x_sc, s + 1)
                    if not first(s, 2):
                        dve.wait_ge(x_lo, s - 1)
                    nc.vector.tensor_scalar(xq[b], xs[b], CLIP, -CLIP, ALU.min, ALU.max).then_inc(x_cl, 1)

                def dve_add(s, b):
                    h = H[:, bass.ds(s, 1), :]
                    for r in range(R):
                        dve.wait_ge(y_mm, s * 3 + r + 1)
                        nc.vector.scalar_tensor_tensor(h[:, :, r * E:(r + 1) * E], ybank[3 * b + r][:, 0:E].unsqueeze(1),
                                                       small[:, 8:9], h[:, :, r * E:(r + 1) * E],
                                                       ALU.mult, ALU.add).then_inc(y_ev, 1)

                def dve_one(s, b):
                    if not (isinstance(s, int) and s == ST - 1):
                        dve_clip(s + 1, 1 - b)
                    if not first(s, 1):
                        dve_add(s - 1, 1 - b)

                dve_clip(0, 0)
                quantised(dve, dve_one)
                dve_add(ST - 1, 1)

            @block.tensor
            def _(pe):
                pe.wait_ge(w_tok, 16)
                pe_embed(pe, 0, 0, 0)
                pe_embed(pe, 0, 0, 1)
                pe.wait_ge(s_const, 1)
                pe.wait_ge(s_one, ONES)
                pe.wait_ge(w_o, 16 * 2)
                iterations(pe, pe_iteration)

                pe.wait_ge(s_ev, 8 * ST)
                pe.wait_ge(p_ev, 8 * ST)
                pe.wait_ge(v_ev, 4 * ST)
                pe.wait_ge(t_ev, 2 * ST)

                def pe_one(s, b):
                    pe.wait_ge(x_lo, s + 1)
                    for r in range(R):
                        if not first(s, 2):
                            pe.wait_ge(y_ev, s * 3 - 5 + r)
                        for w in range(2):
                            for k in range(KT):
                                mm = nc.tensor.matmul(ybank[3 * b + r][:, 0:E],
                                                      xhl[b][:, w, (k * R + r) * P:(k * R + r + 1) * P], wt[:, k, :],
                                                      start=(w == 0 and k == 0), stop=(w == 1 and k == KT - 1))
                        mm.then_inc(y_mm, 1)

                quantised(pe, pe_one)

            @block.sync
            def _(sp):
                sp.dma_start(tw_sb[:], tok_w.rearrange("(k p) n -> p k n", p=P)).then_inc(w_tok, 16)
                load_x(sp, 0, 0)
                sp.dma_start(emb[1][:], tok_b.partition_broadcast(P)).then_inc(w_pos, 16)
                for r, (a, b) in enumerate(((0, 48), (48, 88), (88, 128))):
                    rows = pos[r:16:3, :]
                    sp.dma_start(posb[a:b, :], rows.unsqueeze(1).to_broadcast([(b - a) // 8, 8, E])).then_inc(w_pos, 16)
                load_t(sp, 0, 0)
                sp.dma_start(wq_in.rearrange("p (k n) -> p k n", k=KT), w_qkv.rearrange("(k p) n -> p k n", p=P)).then_inc(w_q, 16)
                load_x(sp, 1, 1)
                sp.dma_start(bq_sb[:], b_qkv.partition_broadcast(P)).then_inc(w_q, 16)
                sp.dma_start(wo_sb[:], w_out.rearrange("(k p) n -> p k n", p=P)).then_inc(w_o, 16)
                sp.dma_start(bo_sb[:], b_out.partition_broadcast(P)).then_inc(w_o, 16)
                place_e(sp, 0, 0)
                sp.dma_start(wf_sb[:], w_ffn.rearrange("(k p) n -> p k n", p=P)).then_inc(w_ffn_in, 16)
                with nc.allow_non_contiguous_dma(reason="256 values"):
                    sp.dma_start(gam[:], ln_gamma.rearrange("(k p) -> p k", p=P)).then_inc(w_ffn_in, 16)
                    sp.dma_start(bet[:], ln_beta.rearrange("(k p) -> p k", p=P)).then_inc(w_ffn_in, 16)
                sp_iteration(sp, -1, 1)
                sp_iteration(sp, 0, 0)
                with sp.Fori(0, (ST - 4) // 2) as i:
                    sp_iteration(sp, i * 2 + 1, 1)
                    sp_iteration(sp, i * 2 + 2, 0)
                sp_iteration(sp, ST - 3, 1, loads_x=False)

                with sp.Fori(0, ST // 2) as i:
                    for b in range(2):
                        s = i * 2 + b
                        sp.wait_ge(y_ev, s * 3 + 3)
                        sp.dma_start(out[bass.ds(s, 1)].rearrange("s p f -> p s f"),
                                     H[:, bass.ds(s, 1), :]).then_inc(st_o[b], 16)
                for b in range(2):
                    sp.wait_ge(st_o[b], 16 * (ST // 2))


def kernel(x, txt, L0_tok_W, L0_tok_b, L0_tok_pos_emb, L0_attn_W_qkv, L0_attn_b_qkv, L0_attn_W_out, L0_attn_b_out,
           L0_ffn_weight, L0_ffn_ln_gamma, L0_ffn_ln_beta):
    import numpy as np
    import concourse.bacc as bacc
    from concourse.bass_utils import run_bass_kernel_spmd

    p = np.ascontiguousarray(x).reshape(ST, 8, 3, 4, 16, 4, 16).transpose(2, 4, 6, 0, 3, 5, 1)
    p = p.reshape(KX, P, ST, 16, 8)
    order = [n for r in range(R) for n in range(r, 16, R)]
    p = np.ascontiguousarray(p[:, :, :, order].transpose(2, 1, 0, 3, 4)).reshape(ST, P, KX * P)
    t = np.ascontiguousarray(txt).reshape(ST, 8, 32 * E)
    whole = np.ascontiguousarray(t[:, :, 2 * E:].reshape(ST, 8, 10, R * E).transpose(0, 2, 1, 3)).reshape(ST, 80, R * E)
    part = np.ascontiguousarray(t[:, :, 0:2 * E])
    arrays = {
        "x_patches": p, "txt_whole": whole, "txt_part": part, "tok_w": np.ascontiguousarray(np.transpose(L0_tok_W)),
        "tok_b": L0_tok_b, "pos": L0_tok_pos_emb, "w_qkv": L0_attn_W_qkv, "b_qkv": L0_attn_b_qkv,
        "w_out": L0_attn_W_out, "b_out": L0_attn_b_out, "w_ffn": L0_ffn_weight, "ln_gamma": L0_ffn_ln_gamma,
        "ln_beta": L0_ffn_ln_beta,
    }
    arrays = {n: np.ascontiguousarray(a) for n, a in arrays.items()}
    nc = bacc.Bacc("TRN2", target_bir_lowering=False, num_devices=1)
    args = [nc.dram_tensor(n, a.shape, mybir.dt.from_np(a.dtype), kind="ExternalInput").ap() for n, a in arrays.items()]
    args.append(nc.dram_tensor("out", (ST, P, R * E), F32, kind="ExternalOutput").ap())
    build(nc, *args)
    got = run_bass_kernel_spmd(nc, [arrays], core_ids=[0]).results[0]["out"]
    return np.ascontiguousarray(np.reshape(got, (ST, 16, 8, R * E)).transpose(0, 2, 1, 3)).reshape(128, 48, E)
```
